# Optimizing a Trainium2 kernel written in Bass

```python
import numpy as np
import jax
import jax.numpy as jnp

def _softmax(x, axis=-1):
    return jax.nn.softmax(x, axis=axis)

def _gelu(x):
    return jax.nn.gelu(x, approximate=True)

def _silu(x):
    return jax.nn.silu(x)

def _sigmoid(x):
    return jax.nn.sigmoid(x)

def _layernorm(x, axis=-1, eps=1e-05):
    m = jnp.mean(x, axis=axis, keepdims=True)
    v = jnp.var(x, axis=axis, keepdims=True)
    return (x - m) / jnp.sqrt(v + eps)

def _scatter_add(tgt, idx, src, axis=0):
    return tgt.at[idx].add(src)

def _segment_sum(src, seg, n):
    return jax.ops.segment_sum(src, seg, n)
kernel_name = 'mk_metaformer_d1_conv_nchw256_r4_9471a0'

def setup_inputs(seed: int=0):
    np.random.seed(seed)
    _w = jnp.asarray

    def _rec_inputs():
        import jax
        import jax.numpy as jnp
        _gk = jax.random.key(seed)
        x = -0.0003929 + 0.9999 * jax.random.normal(jax.random.fold_in(_gk, 1), (16, 64, 16, 16), jnp.float32)
        return x
    x = _rec_inputs()

    def _L0_conv_setup():
        import jax, jax.numpy as jnp
        import numpy as np
        D_MODEL = 64
        EXPAND = 2
        D_INNER = EXPAND * D_MODEL
        HEADDIM = 16
        NHEADS = D_INNER // HEADDIM
        D_STATE = 16
        CONV_DIM = D_INNER + 2 * D_STATE
        D_IN_PROJ = 2 * D_INNER + 2 * D_STATE + NHEADS
        BATCH, HH, WW = (16, 16, 16)
        key = jax.random.key(seed)
        ks = jax.random.split(key, 8)
        u = jax.random.normal(ks[0], (BATCH, D_MODEL, HH, WW), jnp.float32)
        W_in = jax.random.normal(ks[1], (D_IN_PROJ, D_MODEL), jnp.float32) * D_MODEL ** (-0.5)
        conv_w = jax.random.normal(ks[2], (CONV_DIM, 1, 3, 3), jnp.float32) * (1.0 / 3.0)
        conv_b = jnp.zeros((CONV_DIM,), jnp.float32)
        dt = jnp.exp(jax.random.uniform(ks[3], (NHEADS,)) * (np.log(0.1) - np.log(0.001)) + np.log(0.001))
        dt = jnp.clip(dt, 0.0001, None)
        dt_bias = dt + jnp.log(-jnp.expm1(-dt))
        A_log = jnp.log(jax.random.uniform(ks[4], (NHEADS,), minval=1.0, maxval=16.0))
        D = jnp.ones((NHEADS,), jnp.float32)
        ln_g = jnp.ones((D_INNER,), jnp.float32)
        ln_b = jnp.zeros((D_INNER,), jnp.float32)
        W_out = jax.random.normal(ks[5], (D_MODEL, D_INNER), jnp.float32) * D_INNER ** (-0.5)
        return dict(u=u, W_in=W_in, conv_w=conv_w, conv_b=conv_b, dt_bias=dt_bias, A_log=A_log, D=D, ln_g=ln_g, ln_b=ln_b, W_out=W_out, H=HH, W=WW)
    _L0_conv_all = _L0_conv_setup()
    _L0_conv_in = {k: v for k, v in _L0_conv_all.items() if k in ('W_in', 'conv_w', 'conv_b', 'dt_bias', 'A_log', 'D', 'ln_g', 'ln_b', 'W_out')}
    del _L0_conv_all

    def _L0_ffn_setup():
        import jax, jax.numpy as jnp
        import numpy as np
        B, T, D, H, E = (16, 1024, 64, 128, 8)
        key = jax.random.key(seed)
        ks = jax.random.split(key, 5)
        x = jax.random.normal(ks[0], (B, T, D), dtype=jnp.float32)
        gate_w = jax.random.normal(ks[1], (D, E), dtype=jnp.float32) * 0.02
        gate_b = jnp.zeros((E,), dtype=jnp.float32)
        W1 = jax.random.normal(ks[2], (E, D, H), dtype=jnp.float32) * 0.02
        b1 = jnp.zeros((E, H), dtype=jnp.float32)
        W2 = jax.random.normal(ks[3], (E, H, D), dtype=jnp.float32) * 0.02
        b2 = jnp.zeros((E, D), dtype=jnp.float32)
        return {'x': x, 'gate_w': gate_w, 'gate_b': gate_b, 'W1': W1, 'b1': b1, 'W2': W2, 'b2': b2}
    _L0_ffn_all = _L0_ffn_setup()
    _L0_ffn_in = {k: v for k, v in _L0_ffn_all.items() if k in ('gate_w', 'gate_b', 'W1', 'b1', 'W2', 'b2')}
    del _L0_ffn_all
    return {'x': x, 'L0_conv_W_in': _L0_conv_in['W_in'], 'L0_conv_conv_w': _L0_conv_in['conv_w'], 'L0_conv_conv_b': _L0_conv_in['conv_b'], 'L0_conv_dt_bias': _L0_conv_in['dt_bias'], 'L0_conv_A_log': _L0_conv_in['A_log'], 'L0_conv_D': _L0_conv_in['D'], 'L0_conv_ln_g': _L0_conv_in['ln_g'], 'L0_conv_ln_b': _L0_conv_in['ln_b'], 'L0_conv_W_out': _L0_conv_in['W_out'], 'L0_ffn_gate_w': _L0_ffn_in['gate_w'], 'L0_ffn_gate_b': _L0_ffn_in['gate_b'], 'L0_ffn_W1': _L0_ffn_in['W1'], 'L0_ffn_b1': _L0_ffn_in['b1'], 'L0_ffn_W2': _L0_ffn_in['W2'], 'L0_ffn_b2': _L0_ffn_in['b2']}

def reference(x, L0_conv_W_in, L0_conv_conv_w, L0_conv_conv_b, L0_conv_dt_bias, L0_conv_A_log, L0_conv_D, L0_conv_ln_g, L0_conv_ln_b, L0_conv_W_out, L0_ffn_gate_w, L0_ffn_gate_b, L0_ffn_W1, L0_ffn_b1, L0_ffn_W2, L0_ffn_b2):
    import jax
    import jax.numpy as jnp

    def _L0_conv_ref(u, W_in, conv_w, conv_b, dt_bias, A_log, D, ln_g, ln_b, W_out, H, W):
        import jax, jax.numpy as jnp
        import numpy as np
        D_MODEL = 64
        EXPAND = 2
        D_INNER = EXPAND * D_MODEL
        HEADDIM = 16
        NHEADS = D_INNER // HEADDIM
        D_STATE = 16
        CONV_DIM = D_INNER + 2 * D_STATE
        D_IN_PROJ = 2 * D_INNER + 2 * D_STATE + NHEADS
        BATCH, HH, WW = (16, 16, 16)
        B = u.shape[0]
        L = H * W
        x = jnp.transpose(u, (0, 2, 3, 1))
        zxbcdt = jnp.einsum('bhwc,oc->bhwo', x, W_in)
        z = zxbcdt[..., :D_INNER]
        xBC = zxbcdt[..., D_INNER:D_INNER + CONV_DIM]
        dt = jax.nn.softplus(zxbcdt[..., D_INNER + CONV_DIM:] + dt_bias)
        xBC = jnp.transpose(xBC, (0, 3, 1, 2))
        xBC = jax.lax.conv_general_dilated(xBC, conv_w, (1, 1), 'SAME', dimension_numbers=('NCHW', 'OIHW', 'NCHW'), feature_group_count=CONV_DIM) + conv_b[None, :, None, None]
        xBC = jax.nn.silu(xBC)
        xBC = jnp.transpose(xBC, (0, 2, 3, 1)).reshape(B, L, CONV_DIM)
        dt = dt.reshape(B, L, NHEADS)
        z = z.reshape(B, L, D_INNER)
        xs = xBC[..., :D_INNER].reshape(B, L, NHEADS, HEADDIM)
        Bm = xBC[..., D_INNER:D_INNER + D_STATE]
        Cm = xBC[..., D_INNER + D_STATE:]
        A = -jnp.exp(A_log)
        dA = -(dt * A)
        V_scaled = xs * dA[..., None]
        KV = jnp.einsum('bln,blhd->bhnd', Bm, V_scaled)
        y = jnp.einsum('bln,bhnd->blhd', Cm, KV) + xs * D[None, None, :, None]
        y = y.reshape(B, L, D_INNER)
        y = y * jax.nn.silu(z)
        mu = jnp.mean(y, axis=-1, keepdims=True)
        var = jnp.mean(jnp.square(y - mu), axis=-1, keepdims=True)
        y = (y - mu) * jax.lax.rsqrt(var + 1e-05) * ln_g + ln_b
        out = jnp.einsum('bld,od->blo', y, W_out)
        return jnp.transpose(out.reshape(B, H, W, D_MODEL), (0, 3, 1, 2))

    def _L0_ffn_ref(x, gate_w, gate_b, W1, b1, W2, b2):
        import jax, jax.numpy as jnp
        import numpy as np
        B, T, D, H, E = (16, 1024, 64, 128, 8)
        Bb, Tt, Dd = x.shape
        Ee = gate_w.shape[1]
        xf = x.reshape(-1, Dd)
        N = xf.shape[0]
        logits = xf @ gate_w + gate_b
        probs = jax.nn.softmax(logits, axis=-1)
        top2_vals, top2_idx = jax.lax.top_k(probs, 2)
        cw = jnp.zeros((N, Ee), dtype=xf.dtype).at[jnp.arange(N)[:, None], top2_idx].add(top2_vals)

        def step(acc, params):
            w1, bb1, w2, bb2, we = params
            h = jax.nn.gelu(xf @ w1 + bb1, approximate=False)
            y = h @ w2 + bb2
            return (acc + we[:, None] * y, None)
        out, _ = jax.lax.scan(step, jnp.zeros_like(xf), (W1, b1, W2, b2, cw.T))
        return out.reshape(Bb, Tt, Dd)

    def _gn(v, G=32, eps=1e-05):
        B_, C_, H_, W_ = v.shape
        g = v.reshape(B_, G, C_ // G, H_, W_)
        m = jnp.mean(g, axis=(2, 3, 4), keepdims=True)
        s = jnp.var(g, axis=(2, 3, 4), keepdims=True)
        return ((g - m) / jnp.sqrt(s + eps)).reshape(v.shape)

    def _ln_c(v, eps=1e-06):
        m = jnp.mean(v, axis=1, keepdims=True)
        s = jnp.var(v, axis=1, keepdims=True)
        return (v - m) / jnp.sqrt(s + eps)

    def _ln_t(v, eps=1e-05):
        m = jnp.mean(v, axis=-1, keepdims=True)
        s = jnp.var(v, axis=-1, keepdims=True)
        return (v - m) / jnp.sqrt(s + eps)

    def _to_tokens(v):
        B_, C_, H_, W_ = v.shape
        return v.reshape(B_, C_, H_ * W_).transpose(0, 2, 1)

    def _from_tokens(t, like):
        B_, C_, H_, W_ = like.shape
        return t.transpose(0, 2, 1).reshape(B_, C_, H_, W_)
    x = x + _L0_conv_ref(_ln_c(x), L0_conv_W_in, L0_conv_conv_w, L0_conv_conv_b, L0_conv_dt_bias, L0_conv_A_log, L0_conv_D, L0_conv_ln_g, L0_conv_ln_b, L0_conv_W_out, 16, 16)
    t = _to_tokens(x)
    t = t + _L0_ffn_ref(_ln_t(t), L0_ffn_gate_w, L0_ffn_gate_b, L0_ffn_W1, L0_ffn_b1, L0_ffn_W2, L0_ffn_b2)
    x = _from_tokens(t, x)
    return x

_drawn_inputs = setup_inputs


def setup_inputs(seed=0):
    import zlib

    import numpy as np

    out = dict(_drawn_inputs(seed))
    spreads = {'L0_conv_conv_b': (0.0, 0.1),
     'L0_conv_D': (1.0, 0.6),
     'L0_conv_ln_g': (1.0, 0.2),
     'L0_conv_ln_b': (0.0, 0.1),
     'L0_ffn_gate_b': (0.0, 0.653),
     'L0_ffn_b1': (0.0, 0.8),
     'L0_ffn_b2': (0.0, 0.564)}
    factors = {'L0_ffn_gate_w': 5.147, 'L0_ffn_W1': 8.0, 'L0_ffn_W2': 8.0}
    for name, (base, spread) in spreads.items():
        noise = np.random.default_rng([zlib.crc32(name.encode()), seed]).standard_normal(out[name].shape)
        drawn = base * np.exp(spread * noise) if base else spread * noise
        out[name] = jnp.asarray(drawn.astype(out[name].dtype))
    for name, factor in factors.items():
        out[name] = (out[name] * factor).astype(out[name].dtype)
    return out
```

```python
import concourse.bass as bass
from concourse import mybir
from contextlib import ExitStack


class Count:

    def __init__(self, sem, per, base=0):
        self.sem, self.per, self.base = sem, per, base

    def at(self, g, k):
        return g * self.per + k + self.base


def metaformer_block(nc, x, W_in, conv_w, conv_b, dt_bias, A_log, D, ln_g, ln_b, W_out,
                     gate_w, gate_b, W1, b1, W2, b2, out):
    f32, f32r, bf16 = mybir.dt.float32, mybir.dt.float32r, mybir.dt.bfloat16
    ALU, ACT, AX = mybir.AluOpType, mybir.ActivationFunctionType, mybir.AxisListType

    B, C, HH, WW = x.shape
    DI = W_out.shape[1]
    NH = A_log.shape[0]
    HD = DI // NH
    NS = (conv_w.shape[0] - DI) // 2
    E, _, F = W1.shape
    L = HH * WW
    GI = 4
    NG = B // GI
    P = 128
    HT = 2 * L
    TJ = HT // P
    NT = 2 * TJ
    TAPS = 9
    PH, PW = HH + 2, WW + 2
    BC = 2 * NS
    OW = C + 1
    PARTS = 3

    x_v = x.rearrange("(g q b) c h w -> g q c b (h w)", q=2, b=2)
    out_v = out.rearrange("(g q b) c h w -> g q c b (h w)", q=2, b=2)
    cw_v = conv_w.rearrange("o a kh kw -> o (a kh kw)")

    def column(v):
        return v.rearrange("(n a) -> n a", a=1)

    def rows(v, n):
        return v.rearrange("(a n) -> a n", a=1).broadcast_to([n, v.shape[0]])

    ctx = ExitStack()
    with ctx:
        def sb(name, shape, dt=f32):
            return ctx.enter_context(nc.sbuf_tensor(name, shape, dt))

        def sem(name):
            return ctx.enter_context(nc.semaphore(name))

        def count(name, per, base=0):
            return Count(sem(name), per, base)

        ident = sb("ident", [P, P])
        identb = sb("identb", [P, P], bf16)
        wx_raw = sb("wx_raw", [P, C])
        wz_raw = sb("wz_raw", [P, C])
        wbd_raw = sb("wbd_raw", [2 * BC, 2, C])
        cw_x = sb("cw_x", [P, TAPS])
        cb_x = sb("cb_x", [P, 1])
        cw_bc = sb("cw_bc", [P, TAPS])
        cb_bc = sb("cb_bc", [P, 1])
        wo_raw = sb("wo_raw", [C, DI])
        lng = sb("lng", [C, DI])
        lnb = sb("lnb", [DI, 1])
        dskip = sb("dskip", [DI, 1])
        dtb = sb("dtb", [P, NH])
        alog = sb("alog", [P, NH])
        w1_raw = sb("w1_raw", [P, E, F])
        w2 = sb("w2", [F, E, C])
        b1_raw = sb("b1_raw", [E, F])
        b2_raw = sb("b2_raw", [PARTS * E, C])
        gw = sb("gw", [P, E])
        gb = sb("gb", [P, E])
        tapw = sb("tapw", [P, TAPS + 1, C])
        taps_h = sb("taps_h", [P, TAPS + 1, 2, C])
        taps_l = sb("taps_l", [P, TAPS + 1, 2, C])
        wT = sb("wT", [P, TAPS + 1, 2, DI], f32r)
        wbd = sb("wbd", [P, 2 * BC])
        wg = sb("wg", [C, DI])
        wgs = sb("wgs", [C, 1])
        wgc = sb("wgc", [C, DI])
        wo = sb("wo", [DI, OW])
        woT = sb("woT", [DI, C])
        lnbB = sb("lnbB", [DI, P])
        c0 = sb("c0", [P, C])
        expA = sb("expA", [P, NH])
        w1h = sb("w1h", [P, E, F], f32r)
        w1l = sb("w1l", [P, E, F], f32r)
        b1T = sb("b1T", [F, E])
        b2p = sb("b2p", [P, PARTS, C], bf16)
        b2f = sb("b2f", [PARTS * E, 2, C])
        selc = sb("selc", [P, 2, E])
        sel = sb("sel", [P, E, P], bf16)
        rank = sb("rank", [P, E])
        halves = sb("halves", [P, NT])
        xin = sb("xin", [P, HT])
        xtok = sb("xtok", [P, NT, C])
        xpc = sb("xpc", [P, NT, C])
        ln = []
        for n in (1, 2):
            ln.append(dict(
                s1=sb(f"ln{n}_s1", [P, NT]), xc=sb(f"ln{n}_xc", [P, NT, C]), sq=sb(f"ln{n}_sq", [P, NT, C]),
                s2=sb(f"ln{n}_s2", [P, NT]), ve=sb(f"ln{n}_ve", [P, NT]), r=sb(f"ln{n}_r", [P, NT]),
                xn=sb(f"ln{n}_xn", [P, NT, C]), hl=sb(f"ln{n}_hl", [P, NT, 2, C])))
        pad = [sb(f"pad{q}", [P, 2, PH, PW], f32r) for q in range(2)]
        sz = sb("sz", [P, 2, HT])
        xs = sb("xs", [P, 2, HT])
        bcp = sb("bcp", [P, PH, PW])
        bcc = sb("bcc", [P, HH, WW])
        bc = sb("bc", [P, L])
        dtc = sb("dtc", [P, L])
        dtv = sb("dtv", [P, GI * 2, NH])
        dta = sb("dta", [P, GI * 2, NH])
        dtu = sb("dtu", [P, GI * 2, NH])
        dtd = sb("dtd", [P, GI * 2, NH])
        dts = sb("dts", [P, GI * 2, NH])
        dtq = sb("dtq", [P, GI * 2, NH])
        dtp = sb("dtp", [P, GI * 2, NH])
        dA = sb("dA", [P, GI * 2, NH])
        bT = sb("bT", [P, 2, GI, BC])
        v = sb("v", [P, 2, TJ, DI])
        kv = sb("kv", [P, GI, DI])
        gy = sb("gy", [P, 2, HT])
        g = sb("g", [P, 2, HT])
        gsq = sb("gsq", [P, 2, HT])
        gm = sb("gm", [P, TJ, 2])
        gmm = sb("gmm", [P, TJ, 2])
        gv = sb("gv", [P, TJ, 2])
        ge = sb("ge", [P, TJ, 2])
        gr = sb("gr", [P, NT])
        xo = sb("xo", [P, NT, C])
        x2 = sb("x2", [P, NT, C])
        fst = [sb(f"fst{q}", [P, HT], f32r) for q in range(2)]
        ones = sb("ones", [P, 1])
        lg = sb("lg", [P, NT, E])
        m1 = sb("m1", [P, NT])
        ld = sb("ld", [P, NT, E])
        th = sb("th", [P, NT, E])
        tn = sb("tn", [P, NT, E])
        td = sb("td", [P, NT, E])
        pe_ = sb("pe_", [P, NT, E])
        ps_ = sb("ps_", [P, NT])
        pr = sb("pr", [P, NT])
        k1 = sb("k1", [P, NT, E])
        kk = sb("kk", [P, NT])
        o1 = sb("o1", [P, NT, E])
        lg2 = sb("lg2", [P, NT, E])
        o2 = sb("o2", [P, NT, E])
        cw = sb("cw", [P, NT, E])
        cr = sb("cr", [P, 2, NT, E])
        cwp = sb("cwp", [P, NT, P], bf16)
        cwT = sb("cwT", [P, 2, HT], bf16)
        bst = [sb(f"bst{q}", [P, HT], f32r) for q in range(2)]
        bcw = sb("bcw", [P, 2, HT], bf16)
        bx2 = sb("bx2", [P, NT, C])
        hid = sb("hid", [P, 2, HT])
        hw = [sb(f"hw{k}", [P, 2, HT]) for k in range(2)]
        ost = sb("ost", [P, HT])

        pf = ctx.enter_context(nc.psum_tensor("pf", [P, 4, HT], f32))
        ph = [ctx.enter_context(nc.psum_tensor(f"ph{q}", [P, HT], f32)) for q in range(2)]
        pc = ctx.enter_context(nc.psum_tensor("pc", [P, HT], f32))
        pa = ctx.enter_context(nc.psum_tensor("pa", [P, HT], f32))

        d_proj = sem("d_proj")
        d_bc = sem("d_bc")
        d_mix = sem("d_mix")
        d_exp = sem("d_exp")
        d_wbd = sem("d_wbd")
        d_dt = sem("d_dt")
        MIX, CONV, EXP = 5, 1 + 2 * GI, 6 + PARTS
        POOL_ALL, ACT_ALL = 13 + E, 9
        i_pool = sem("i_pool")
        i_dve = sem("i_dve")
        i_pe = sem("i_pe")
        i_act = sem("i_act")
        x_in = count("x_in", 32)
        x_out = count("x_out", 32, 1)
        turned = count("turned", 1)
        kept = count("kept", 1)
        xpc_in = count("xpc_in", 1)
        ln_dve = [count(f"ln{n}_dve", 6) for n in (1, 2)]
        ln_sq = [count(f"ln{n}_sqd", 1) for n in (1, 2)]
        ln_pow = [count(f"ln{n}_pow", 1) for n in (1, 2)]
        ln_high = [count(f"ln{n}_high", 1) for n in (1, 2)]
        split = [count(f"split{n}", 2) for n in (1, 2)]
        padded = [count(f"padded{q}", 1) for q in range(2)]
        bd = count("bd", 1)
        bcp_in = count("bcp_in", 1)
        dtc_in = count("dtc_in", 1)
        dt_t = count("dt_t", 1)
        dt_dve = count("dt_dve", 16)
        dt_exp = count("dt_exp", 1)
        bc_conv = count("bc_conv", TAPS)
        bc_in = count("bc_in", 1)
        zx = count("zx", 4)
        zx_up = count("zx_up", 4)
        bT_t = count("bT_t", 1)
        bT_in = count("bT_in", 1)
        xs_t = count("xs_t", 2)
        v_in = count("v_in", 2)
        kv_ps = count("kv_ps", 2)
        kv_in = count("kv_in", GI)
        y_ps = count("y_ps", 2)
        y_dve = count("y_dve", 4)
        gsq_in = count("gsq_in", 2)
        o_ps = count("o_ps", 2)
        o_dve = count("o_dve", 6)
        o_pow = count("o_pow", 1)
        fst_in = [count(f"fst_in{q}", 1) for q in range(2)]
        gate_ps = count("gate_ps", 1)
        rt = count("rt", 25)
        rt_tanh = count("rt_tanh", 1)
        cw_t = count("cw_t", 1)
        cwT_in = count("cwT_in", 1)
        over = count("over", 4)
        hid_ps = count("hid_ps", 2 * E)
        hid_in = count("hid_in", 2 * E, 1)
        cwb = count("cwb", 2 * E)
        hw_in = count("hw_in", 2 * E, 1)
        done = count("done", E, 1)
        ost_in = count("ost_in", 1, 1)

        BREAK = 9
        PLAN = [("back", 0), ("mixer", "turn"), ("back", 1), ("back", 2), ("mixer", "var1"), ("back", 3), ("back", 4),
                ("mixer", "norm1"), ("back", 5), ("back", 6), ("mixer", "split1"), ("back", 7), ("back", 8),
                ("mixer", "bd"), ("mixer", "conv"), ("router", "output"), ("mixer", "x0"), ("router", "residual"),
                ("mixer", "z0"), ("mixer", "x1"), ("router", "var2"), ("router", "norm2"), ("router", "split2"),
                ("mixer", "z1"), ("router", "gate"), ("mixer", "tokens0"), ("mixer", "tokens1"), ("router", "route"),
                ("back", 9), ("mixer", "states0"), ("back", 10), ("router", "route2"), ("back", 11),
                ("mixer", "states1"), ("back", 12), ("router", "weights"), ("back", 13), ("back", 14), ("back", 15)]

        def run(eng, front, back, end, once=lambda step: None):
            for part, step in PLAN:
                if part == "mixer":
                    front(step, 0)
                    once(step)
            for part, step in PLAN:
                if part != "back":
                    front(step, 0 if part == "router" else 1)
            end(None, 0)
            with eng.Fori(0, NG - 2) as i:
                for part, step in PLAN:
                    if part == "back":
                        back(step // 2, step % 2, i)
                    else:
                        front(step, i + 1 if part == "router" else i + 2)
                end(i, i + 1)
            for part, step in PLAN:
                if part == "back":
                    back(step // 2, step % 2, NG - 2)
                elif part == "router":
                    front(step, NG - 1)
            end(NG - 2, NG - 1)
            for u in range(2 * E):
                back(u // 2, u % 2, NG - 1)
            end(NG - 1, None)

        def later(eng, c, grp, k):
            if not (isinstance(grp, int) and grp == 0):
                eng.wait_ge(c.sem, c.at(grp - 1, k))

        def first(grp):
            return isinstance(grp, int) and grp == 0

        def interior(t):
            return t[:, :, 1:1 + HH, 1:1 + WW]

        block = ctx.enter_context(nc.Block())

        @block.sync
        def _(sp):
            sp.sem_inc(x_out.sem, 1)

            def load(grp):
                later(sp, turned, grp, 1)
                for q in range(2):
                    sp.dma_start(xin[C * q:C * q + C, :].rearrange("c (b l) -> c b l", b=2),
                                 x_v[grp, q]).then_inc(x_in.sem, 16)

            load(0)
            sp.dma_start(wx_raw[:], W_in[DI:2 * DI, :]).then_inc(d_proj, 16)
            sp.dma_start(cw_x[:], cw_v[0:DI, :]).then_inc(d_proj, 16)
            sp.dma_start(wz_raw[:], W_in[0:DI, :]).then_inc(d_proj, 16)
            sp.wait_ge(i_pool, 1)
            sp.dma_start(wbd_raw[0:BC + NH, :, :],
                         W_in[2 * DI:2 * DI + BC + NH, :].unsqueeze(1).broadcast_to([BC + NH, 2, C])).then_inc(d_wbd, 16)
            sp.dma_start(dtb[:], rows(dt_bias, P)).then_inc(d_dt, 16)
            sp.dma_start(alog[:], rows(A_log, P)).then_inc(d_dt, 16)
            for i in range(GI):
                sp.dma_start(cw_bc[BC * i:BC * i + BC, :], cw_v[DI:DI + BC, :]).then_inc(d_bc, 16)
            for i in range(GI):
                sp.dma_start(cb_bc[BC * i:BC * i + BC, :], column(conv_b)[DI:DI + BC, :]).then_inc(d_bc, 16)
            sp.dma_start(cb_x[:], column(conv_b)[0:DI, :]).then_inc(d_bc, 16)
            sp.dma_start(wo_raw[:], W_out).then_inc(d_mix, 16)
            sp.dma_start(lng[:], rows(ln_g, C)).then_inc(d_mix, 16)
            sp.dma_start(lnb[:], column(ln_b)).then_inc(d_mix, 16)
            sp.dma_start(dskip[:], column(D).unsqueeze(1).broadcast_to([NH, HD, 1])).then_inc(d_mix, 16)
            sp.dma_start(b1_raw[:], b1).then_inc(d_mix, 16)
            load(1)
            sp.dma_start(gb[:], rows(gate_b, P)).then_inc(d_exp, 16)
            for r in range(2):
                sp.dma_start(gw[C * r:C * r + C, :], gate_w).then_inc(d_exp, 16)
            for r in range(2):
                sp.dma_start(w1_raw[C * r:C * r + C, :, :], W1.rearrange("e c f -> c e f")).then_inc(d_exp, 16)
            for r in range(PARTS):
                sp.dma_start(b2_raw[E * r:E * r + E, :], b2).then_inc(d_exp, 16)
            sp.dma_start(w2[:], W2.rearrange("e f c -> f e c")).then_inc(d_exp, 16)

            def store(grp):
                sp.wait_ge(ost_in.sem, ost_in.at(grp, 1))
                for q in range(2):
                    sp.dma_start(out_v[grp, q],
                                 ost[C * q:C * q + C, :].rearrange("c (b l) -> c b l", b=2)).then_inc(x_out.sem, 16)

            with sp.Fori(0, NG - 2) as i:
                load(i + 2)
                store(i)
            for grp in range(NG - 2, NG):
                store(grp)
            sp.wait_ge(x_out.sem, x_out.at(NG - 1, 32))

        @block.gpsimd
        def _(pool):
            pool.memset(wbd_raw[:], 0.0).then_inc(i_pool, 1)
            pool.memset(ident[:], 0.0).then_inc(i_pool, 1)
            pool.wait_ge(i_pool, 2)
            pool.affine_select(out=ident[:], in_=ident[:], compare_op=ALU.not_equal, fill=1.0, base=0,
                               pattern=[[-1, P]], channel_multiplier=1).then_inc(i_pool, 1)
            pool.memset(halves[:], -0.5).then_inc(i_pool, 1)
            pool.memset(pad[0][:].bitcast(f32), 0.0).then_inc(i_pool, 1)
            pool.memset(pad[1][:].bitcast(f32), 0.0).then_inc(i_pool, 1)
            pool.memset(bcp[:], 0.0).then_inc(i_pool, 1)
            pool.memset(bT[:], 0.0).then_inc(i_pool, 1)
            pool.memset(kv[:], 0.0).then_inc(i_pool, 1)
            pool.wait_ge(i_pool, 4)

            def once(step):
                if step == "var1":
                    pool.memset(cwp[:], 0.0).then_inc(i_pool, 1)
                    pool.memset(b2p[:], 0.0).then_inc(i_pool, 1)
                    pool.memset(ones[:], 1.0 / DI).then_inc(i_pool, 1)
                    for e in range(E):
                        pool.memset(rank[:, e:e + 1], float(E - e)).then_inc(i_pool, 1)
                    pool.tensor_copy(identb[:], ident[:]).then_inc(i_pool, 1)

            def power(n, grp):
                pool.wait_ge(ln_dve[n].sem, ln_dve[n].at(grp, 4))
                pool.tensor_tensor(ln[n]["r"][:], ln[n]["ve"][:], halves[:], ALU.pow).then_inc(ln_pow[n].sem, 1)

            def front(step, grp):
                if step == "var1":
                    power(0, grp)
                elif step == "var2":
                    power(1, grp)
                elif step == "states1":
                    pool.wait_ge(kept.sem, kept.at(grp, 1))
                    if first(grp):
                        pool.wait_ge(i_act, ACT_ALL)
                    later(pool, o_dve, grp, 6)
                    pool.tensor_tensor(xpc[:], xtok[:], c0[:].unsqueeze(1).broadcast_to([P, NT, C]),
                                       ALU.add).then_inc(xpc_in.sem, 1)
                elif step == "output":
                    pool.wait_ge(o_dve.sem, o_dve.at(grp, 4))
                    pool.tensor_tensor(gr[:], ge[:].rearrange("p j q -> p (j q)"), halves[:],
                                       ALU.pow).then_inc(o_pow.sem, 1)

            run(pool, front, lambda e, q, grp: None, lambda grp, nxt: None, once)

        @block.scalar
        def _(act):
            act.sem_inc(hid_in.sem, 1)
            act.sem_inc(ost_in.sem, 1)

            def once(step):
                if step == "turn":
                    for n, bank in ((1, ph[1]), (3, pa)):
                        act.wait_ge(i_pe, n + 1)
                        act.activation(wT[:, 2 * n:2 * n + 2, :, :].rearrange("p t s o -> p (t s o)"), bank[:],
                                       ACT.Copy).then_inc(i_act, 1)
                    act.wait_ge(i_pe, 6)
                    act.activation(wbd[:], pf[:, 1, 0:2 * BC], ACT.Copy).then_inc(i_act, 1)
                elif step == "bd":
                    act.wait_ge(d_dt, 16 * 2)
                    act.activation(expA[:], alog[:], ACT.Exp).then_inc(i_act, 1)
                elif step == "z0":
                    act.wait_ge(i_pe, 7)
                    act.activation(wo[:, 0:C], pf[:, 0, 0:C], ACT.Copy).then_inc(i_act, 1)
                    act.activation(woT[:], pf[:, 0, C:2 * C], ACT.Copy).then_inc(i_act, 1)
                    act.activation(b1T[:], pf[:, 0, 2 * C:2 * C + E], ACT.Copy).then_inc(i_act, 1)
                elif step == "x1":
                    act.wait_ge(i_pe, 8)
                    act.activation(c0[:], pa[:, 0:C], ACT.Copy).then_inc(i_act, 1)
                elif step == "states1":
                    act.wait_ge(d_exp, 16 * EXP)
                    act.activation(w1h[:], w1_raw[:], ACT.Copy).then_inc(i_act, 1)

            def square(n, grp):
                act.wait_ge(ln_dve[n].sem, ln_dve[n].at(grp, 2))
                act.activation(ln[n]["sq"][:], ln[n]["xc"][:], ACT.Square).then_inc(ln_sq[n].sem, 1)

            def high(n, grp):
                act.wait_ge(ln_dve[n].sem, ln_dve[n].at(grp, 5))
                later(act, split[n], grp, 2)
                act.activation(ln[n]["hl"][:, :, 0, :].bitcast(f32r), ln[n]["xn"][:], ACT.Copy)\
                   .then_inc(ln_high[n].sem, 1)

            def silu(k, out_, bank, bias, grp):
                act.wait_ge(zx.sem, zx.at(grp, k))
                later(act, y_dve, grp, 4)
                act.activation(out_, bank, ACT.Silu, bias=bias).then_inc(zx_up.sem, 1)

            def states(q, grp):
                act.wait_ge(kv_ps.sem, kv_ps.at(grp, q + 1))
                later(act, y_ps, grp, 2)
                for i in (2 * q, 2 * q + 1):
                    rws = slice(BC * i, BC * i + BC)
                    act.activation(kv[rws, i, :], pf[rws, 2, 0:DI], ACT.Copy).then_inc(kv_in.sem, 1)
                act.wait_ge(y_dve.sem, y_dve.at(grp, 2 * q + 2))
                later(act, o_ps, grp, 2)
                act.activation(gsq[:, q, :], g[:, q, :], ACT.Square).then_inc(gsq_in.sem, 1)

            def front(step, grp):
                if step == "turn":
                    act.wait_ge(turned.sem, turned.at(grp, 1))
                    later(act, xpc_in, grp, 1)
                    act.activation(xtok[:].rearrange("p t c -> p (t c)"), pf[:, 2, :], ACT.Copy).then_inc(kept.sem, 1)
                    square(0, grp)
                elif step == "residual":
                    square(1, grp)
                elif step == "norm1":
                    high(0, grp)
                elif step == "norm2":
                    high(1, grp)
                elif step == "split1":
                    act.wait_ge(split[0].sem, split[0].at(grp, 1))
                    if first(grp):
                        act.wait_ge(i_pool, 9)
                    later(act, zx, grp, 4)
                    act.activation(interior(pad[0]), pf[:, 2, :].rearrange("p (b h w) -> p b h w", b=2, h=HH),
                                   ACT.Copy).then_inc(padded[0].sem, 1)
                elif step == "bd":
                    act.wait_ge(dt_dve.sem, dt_dve.at(grp, 2))
                    act.activation(dtu[:], dta[:], ACT.Exp, scale=-1.0).then_inc(dt_exp.sem, 1)
                elif step == "conv":
                    if first(grp):
                        act.wait_ge(d_bc, 16 * CONV)
                    act.wait_ge(bc_conv.sem, bc_conv.at(grp, TAPS))
                    later(act, y_ps, grp, 2)
                    act.activation(bc[:], bcc[:].rearrange("p h w -> p (h w)"), ACT.Silu,
                                   bias=cb_bc[:, 0:1]).then_inc(bc_in.sem, 1)
                elif step == "split2":
                    act.wait_ge(split[1].sem, split[1].at(grp, 1))
                    later(act, over, grp, 3)
                    act.activation(fst[0][:], pf[:, 0, :], ACT.Copy).then_inc(fst_in[0].sem, 1)
                elif step == "x0":
                    silu(1, xs[:, 0, :], ph[0][:], cb_x[:, 0:1], grp)
                elif step == "z0":
                    silu(2, sz[:, 0, :], pf[:, 2, :], 0.0, grp)
                elif step == "route":
                    act.wait_ge(rt.sem, rt.at(grp, 3))
                    act.activation(th[:], ld[:], ACT.Tanh, scale=0.5).then_inc(rt_tanh.sem, 1)
                elif step == "tokens0":
                    act.wait_ge(bT_t.sem, bT_t.at(grp, 1))
                    later(act, kv_ps, grp, 2)
                    act.activation(bT[:, :, :, NS:BC],
                                   pf[:, 2, 0:L].rearrange("p (t i n) -> p t i n", t=2, i=GI)[:, :, :, 0:NS],
                                   ACT.Copy).then_inc(bT_in.sem, 1)
                elif step == "x1":
                    silu(3, xs[:, 1, :], ph[1][:], cb_x[:, 0:1], grp)
                elif step == "states0":
                    states(0, grp)
                elif step == "z1":
                    silu(4, sz[:, 1, :], pc[:], 0.0, grp)
                elif step == "states1":
                    states(1, grp)

            def back(e, q, grp):
                n = 2 * e + q
                act.wait_ge(hid_ps.sem, hid_ps.at(grp, n + 1))
                act.wait_ge(hw_in.sem, hw_in.at(grp, max(n - 1, 0)))
                act.activation(hid[:, q, :], ph[q][:], ACT.Gelu, bias=b1T[:, e:e + 1]).then_inc(hid_in.sem, 1)

            def end(grp, nxt):
                if grp is not None:
                    act.wait_ge(done.sem, done.at(grp, E))
                    act.wait_ge(x_out.sem, x_out.at(grp, 0))
                    act.activation(ost[:], pa[:], ACT.Copy).then_inc(ost_in.sem, 1)

            run(act, front, back, end, once)

        @block.vector
        def _(dve):
            dve.sem_inc(hw_in.sem, 1)

            def bcast(t, n):
                return t.unsqueeze(2).broadcast_to([P, t.shape[1], n])

            def once(step):
                if step == "turn":
                    dve.wait_ge(d_proj, 16 * 3)
                    for t in range(TAPS):
                        dve.tensor_scalar(tapw[:, t, :], wx_raw[:], cw_x[:, t:t + 1], None, ALU.mult).then_inc(i_dve, 1)
                    dve.tensor_copy(tapw[:, TAPS, :], wz_raw[:]).then_inc(i_dve, 1)
                    dve.wait_ge(i_dve, 10)
                    for r in range(2):
                        dve.tensor_copy(taps_h[:, :, r, :].bitcast(f32r), tapw[:]).then_inc(i_dve, 1)
                elif step == "var1":
                    dve.wait_ge(i_dve, 12)
                    for r in range(2):
                        dve.tensor_tensor(taps_l[:, :, r, :], tapw[:], taps_h[:, :, r, :], ALU.subtract)\
                           .then_inc(i_dve, 1)
                elif step == "norm1":
                    for n, bank in ((0, ph[0][:]), (2, pc[:]), (4, pf[:, 0, :])):
                        dve.wait_ge(i_pe, n + 1)
                        dve.tensor_copy(wT[:, 2 * n:2 * n + 2, :, :].rearrange("p t s o -> p (t s o)"),
                                        bank).then_inc(i_dve, 1)
                elif step == "conv":
                    dve.wait_ge(d_mix, 16 * MIX)
                    dve.tensor_tensor(wg[:], wo_raw[:], lng[:], ALU.mult).then_inc(i_dve, 1)
                    dve.wait_ge(i_dve, 18)
                    dve.reduce_sum(wgs[:], wg[:], axis=AX.X).then_inc(i_dve, 1)
                    dve.wait_ge(i_dve, 19)
                    dve.scalar_tensor_tensor(out=wgc[:], in0=wgs[:, 0:1].broadcast_to([C, DI]), scalar=-1.0 / DI,
                                             in1=wg[:], op0=ALU.mult, op1=ALU.add).then_inc(i_dve, 1)
                    dve.tensor_copy(lnbB[:], lnb[:, 0:1].broadcast_to([DI, P])).then_inc(i_dve, 1)
                    dve.memset(wo[:, C:OW], 1.0 / DI).then_inc(i_dve, 1)
                elif step == "states1":
                    dve.wait_ge(i_pool, POOL_ALL)
                    dve.tensor_tensor(selc[:, 0], ident[:, 0:E], ident[:, E:2 * E], ALU.add).then_inc(i_dve, 1)
                    dve.wait_ge(i_dve, 23)
                    dve.tensor_tensor(selc[:, 1], selc[:, 0], ident[:, 2 * E:3 * E], ALU.add).then_inc(i_dve, 1)
                    dve.wait_ge(i_dve, 24)
                    dve.tensor_copy(sel[:], selc[:, 1].unsqueeze(2).broadcast_to([P, E, P])).then_inc(i_dve, 1)
                    dve.wait_ge(d_exp, 16 * EXP)
                    dve.wait_ge(i_act, 9)
                    dve.tensor_tensor(w1l[:], w1_raw[:], w1h[:].bitcast(f32), ALU.subtract).then_inc(i_dve, 1)
                    R = PARTS * E
                    dve.tensor_copy(b2p[0:R, 0, :], b2_raw[:]).then_inc(i_dve, 1)
                    dve.wait_ge(i_dve, 27)
                    dve.tensor_tensor(b2f[:, 0], b2_raw[:], b2p[0:R, 0, :], ALU.subtract).then_inc(i_dve, 1)
                    dve.wait_ge(i_dve, 28)
                    dve.tensor_copy(b2p[0:R, 1, :], b2f[:, 0]).then_inc(i_dve, 1)
                    dve.wait_ge(i_dve, 29)
                    dve.tensor_tensor(b2f[:, 1], b2f[:, 0], b2p[0:R, 1, :], ALU.subtract).then_inc(i_dve, 1)
                    dve.wait_ge(i_dve, 30)
                    dve.tensor_copy(b2p[0:R, 2, :], b2f[:, 1]).then_inc(i_dve, 1)

            def centre(n, grp, src):
                t, c = ln[n], ln_dve[n]
                dve.reduce_sum(t["s1"][:], src, axis=AX.X).then_inc(c.sem, 1)
                later(dve, ln_sq[n], grp, 1)
                dve.wait_ge(c.sem, c.at(grp, 1))
                dve.scalar_tensor_tensor(out=t["xc"][:], in0=bcast(t["s1"][:], C), scalar=-1.0 / C, in1=src,
                                         op0=ALU.mult, op1=ALU.add).then_inc(c.sem, 1)

            def variance(n, grp):
                t, c = ln[n], ln_dve[n]
                dve.wait_ge(ln_sq[n].sem, ln_sq[n].at(grp, 1))
                dve.reduce_sum(t["s2"][:], t["sq"][:], axis=AX.X).then_inc(c.sem, 1)
                dve.wait_ge(c.sem, c.at(grp, 3))
                dve.tensor_scalar(t["ve"][:], t["s2"][:], 1.0 / C, 1e-6 if n == 0 else 1e-5,
                                  ALU.mult, ALU.add).then_inc(c.sem, 1)

            def normalise(n, grp):
                t, c = ln[n], ln_dve[n]
                dve.wait_ge(ln_pow[n].sem, ln_pow[n].at(grp, 1))
                dve.tensor_tensor(t["xn"][:], t["xc"][:], bcast(t["r"][:], C), ALU.mult).then_inc(c.sem, 1)
                dve.wait_ge(ln_high[n].sem, ln_high[n].at(grp, 1))
                dve.tensor_tensor(t["hl"][:, :, 1, :], t["xn"][:], t["hl"][:, :, 0, :], ALU.subtract).then_inc(c.sem, 1)

            def conv_and_softplus(grp):
                c = dt_dve

                def tap(t):
                    view = bcp[:, t // 3:t // 3 + HH, t % 3:t % 3 + WW]
                    if t == 0:
                        ins = dve.tensor_scalar(bcc[:], view, cw_bc[:, 0:1], None, ALU.mult)
                    else:
                        dve.wait_ge(bc_conv.sem, bc_conv.at(grp, t))
                        ins = dve.scalar_tensor_tensor(out=bcc[:], in0=view, scalar=cw_bc[:, t:t + 1], in1=bcc[:],
                                                       op0=ALU.mult, op1=ALU.add)
                    ins.then_inc(bc_conv.sem, 1)

                dve.wait_ge(bcp_in.sem, bcp_in.at(grp, 1))
                later(dve, bc_in, grp, 1)
                if first(grp):
                    dve.wait_ge(d_bc, 16 * CONV)
                tap(0)
                dve.wait_ge(dt_exp.sem, dt_exp.at(grp, 1))
                dve.tensor_scalar(dtd[:], dtu[:], 2.0, None, ALU.add).then_inc(c.sem, 1)
                tap(1)
                dve.wait_ge(c.sem, c.at(grp, 3))
                dve.reciprocal(dtd[:], dtd[:]).then_inc(c.sem, 1)
                tap(2)
                dve.wait_ge(c.sem, c.at(grp, 4))
                dve.tensor_tensor(dts[:], dtu[:], dtd[:], ALU.mult).then_inc(c.sem, 1)
                tap(3)
                dve.wait_ge(c.sem, c.at(grp, 5))
                dve.tensor_tensor(dtq[:], dts[:], dts[:], ALU.mult).then_inc(c.sem, 1)
                tap(4)
                dve.wait_ge(c.sem, c.at(grp, 6))
                dve.tensor_scalar(dtp[:], dtq[:], 1.0 / 13.0, None, ALU.mult).then_inc(c.sem, 1)
                for k, m in enumerate((11, 9, 7, 5, 3)):
                    if 5 + k < TAPS:
                        tap(5 + k)
                    dve.wait_ge(c.sem, c.at(grp, 7 + k))
                    dve.scalar_tensor_tensor(out=dtp[:], in0=dtp[:], scalar=1.0 / m, in1=dtq[:],
                                             op0=ALU.add, op1=ALU.mult).then_inc(c.sem, 1)
                dve.tensor_scalar(dtv[:], dtv[:], 0.0, None, ALU.max).then_inc(c.sem, 1)
                dve.wait_ge(c.sem, c.at(grp, 12))
                dve.scalar_tensor_tensor(out=dtp[:], in0=dtp[:], scalar=1.0, in1=dts[:],
                                         op0=ALU.add, op1=ALU.mult).then_inc(c.sem, 1)
                dve.wait_ge(c.sem, c.at(grp, 14))
                dve.scalar_tensor_tensor(out=dtp[:], in0=dtp[:], scalar=2.0, in1=dtv[:],
                                         op0=ALU.mult, op1=ALU.add).then_inc(c.sem, 1)
                if first(grp):
                    dve.wait_ge(i_act, 4)
                dve.wait_ge(c.sem, c.at(grp, 15))
                dve.tensor_tensor(dA[:], dtp[:], expA[:].unsqueeze(1).broadcast_to([P, GI * 2, NH]),
                                  ALU.mult).then_inc(c.sem, 1)

            def route(grp):
                rankB = rank[:].unsqueeze(1).broadcast_to([P, NT, E])

                def after(k):
                    dve.wait_ge(rt.sem, rt.at(grp, k))

                dve.wait_ge(gate_ps.sem, gate_ps.at(grp, 1))
                dve.tensor_tensor(lg[:], pf[:, 1, 0:NT * E].rearrange("p (t e) -> p t e", e=E),
                                  gb[:].unsqueeze(1).broadcast_to([P, NT, E]), ALU.add).then_inc(rt.sem, 1)
                after(1)
                dve.reduce_max(m1[:], lg[:], axis=AX.X).then_inc(rt.sem, 1)
                after(2)
                dve.tensor_tensor(ld[:], lg[:], bcast(m1[:], E), ALU.subtract).then_inc(rt.sem, 1)
                after(3)
                dve.scalar_tensor_tensor(out=k1[:], in0=ld[:], scalar=0.0, in1=rankB,
                                         op0=ALU.is_ge, op1=ALU.mult).then_inc(rt.sem, 1)
                after(4)
                dve.reduce_max(kk[:], k1[:], axis=AX.X).then_inc(rt.sem, 1)
                dve.wait_ge(rt_tanh.sem, rt_tanh.at(grp, 1))
                dve.tensor_scalar(td[:], th[:], -1.0, 1.0, ALU.mult, ALU.add).then_inc(rt.sem, 1)
                after(5)
                dve.tensor_tensor(o1[:], k1[:], bcast(kk[:], E), ALU.is_equal).then_inc(rt.sem, 1)
                after(6)
                dve.reciprocal(td[:], td[:]).then_inc(rt.sem, 1)
                after(7)
                dve.scalar_tensor_tensor(out=lg2[:], in0=o1[:], scalar=-1e30, in1=ld[:],
                                         op0=ALU.mult, op1=ALU.add).then_inc(rt.sem, 1)
                after(8)
                dve.scalar_tensor_tensor(out=pe_[:], in0=th[:], scalar=1.0, in1=td[:],
                                         op0=ALU.add, op1=ALU.mult).then_inc(rt.sem, 1)
                after(9)
                dve.reduce_max(m1[:], lg2[:], axis=AX.X).then_inc(rt.sem, 1)
                after(10)
                dve.reduce_sum(ps_[:], pe_[:], axis=AX.X).then_inc(rt.sem, 1)
                after(11)
                dve.tensor_tensor(lg2[:], lg2[:], bcast(m1[:], E), ALU.subtract).then_inc(rt.sem, 1)
                after(12)
                dve.reciprocal(pr[:], ps_[:]).then_inc(rt.sem, 1)

            def route2(grp):
                rankB = rank[:].unsqueeze(1).broadcast_to([P, NT, E])

                def after(k):
                    dve.wait_ge(rt.sem, rt.at(grp, k))

                after(13)
                dve.scalar_tensor_tensor(out=k1[:], in0=lg2[:], scalar=0.0, in1=rankB,
                                         op0=ALU.is_ge, op1=ALU.mult).then_inc(rt.sem, 1)
                after(14)
                dve.tensor_tensor(pe_[:], pe_[:], bcast(pr[:], E), ALU.mult).then_inc(rt.sem, 1)
                after(15)
                dve.reduce_max(kk[:], k1[:], axis=AX.X).then_inc(rt.sem, 1)
                after(17)
                dve.tensor_tensor(o2[:], k1[:], bcast(kk[:], E), ALU.is_equal).then_inc(rt.sem, 1)
                after(18)
                dve.tensor_tensor(o1[:], o1[:], o2[:], ALU.add).then_inc(rt.sem, 1)
                after(19)
                dve.tensor_tensor(cw[:], pe_[:], o1[:], ALU.mult).then_inc(rt.sem, 1)
                after(20)
                if first(grp):
                    dve.wait_ge(i_pool, POOL_ALL)
                dve.tensor_copy(cwp[:, :, 0:E], cw[:]).then_inc(rt.sem, 1)
                after(21)
                dve.tensor_tensor(cr[:, 0], cw[:], cwp[:, :, 0:E], ALU.subtract).then_inc(rt.sem, 1)
                after(22)
                dve.tensor_copy(cwp[:, :, E:2 * E], cr[:, 0]).then_inc(rt.sem, 1)
                after(23)
                dve.tensor_tensor(cr[:, 1], cr[:, 0], cwp[:, :, E:2 * E], ALU.subtract).then_inc(rt.sem, 1)
                after(24)
                dve.tensor_copy(cwp[:, :, 2 * E:3 * E], cr[:, 1]).then_inc(rt.sem, 1)

            def tokens(q, bank, grp):
                dve.wait_ge(dt_dve.sem, dt_dve.at(grp, 16))
                dve.wait_ge(xs_t.sem, xs_t.at(grp, q + 1))
                later(dve, kv_ps, grp, 2)
                dve.tensor_tensor(
                    v[:, q].rearrange("p j (h d) -> p (j h) d", d=HD),
                    pf[:, bank, :].rearrange("p (n d) -> p n d", d=HD),
                    dA[:, 4 * q:4 * q + 4, :].rearrange("p a h -> p (a h)").unsqueeze(2)
                    .broadcast_to([P, TJ * NH, HD]), ALU.mult).then_inc(v_in.sem, 1)

            def states(q, bank, grp):
                dve.wait_ge(y_ps.sem, y_ps.at(grp, q + 1))
                dve.scalar_tensor_tensor(out=gy[:, q, :], in0=xs[:, q, :], scalar=dskip[:, 0:1], in1=pf[:, bank, :],
                                         op0=ALU.mult, op1=ALU.add).then_inc(y_dve.sem, 1)
                dve.wait_ge(y_dve.sem, y_dve.at(grp, 2 * q + 1))
                dve.wait_ge(zx_up.sem, zx_up.at(grp, 2 * q + 2))
                later(dve, o_ps, grp, 2)
                dve.tensor_tensor(g[:, q, :], gy[:, q, :], sz[:, q, :], ALU.mult).then_inc(y_dve.sem, 1)

            def front(step, grp):
                if step == "turn":
                    dve.wait_ge(kept.sem, kept.at(grp, 1))
                    centre(0, grp, xtok[:])
                elif step == "var1":
                    variance(0, grp)
                elif step == "var2":
                    variance(1, grp)
                elif step == "norm1":
                    normalise(0, grp)
                elif step == "norm2":
                    normalise(1, grp)
                elif step == "split1":
                    dve.wait_ge(split[0].sem, split[0].at(grp, 2))
                    if first(grp):
                        dve.wait_ge(i_pool, 9)
                    later(dve, zx, grp, 4)
                    dve.tensor_copy(interior(pad[1]), pf[:, 3, :].rearrange("p (b h w) -> p b h w", b=2, h=HH))\
                       .then_inc(padded[1].sem, 1)
                elif step == "bd":
                    dve.wait_ge(bd.sem, bd.at(grp, 1))
                    later(dve, dt_t, grp, 1)
                    dve.tensor_copy(dtc[:], pf[:, 2, L:2 * L]).then_inc(dtc_in.sem, 1)
                    dve.tensor_copy(bcp[:, 1:1 + HH, 1:1 + WW],
                                    pf[:, 2, 0:L].rearrange("p (h w) -> p h w", h=HH)).then_inc(bcp_in.sem, 1)
                    dve.wait_ge(dt_t.sem, dt_t.at(grp, 1))
                    if first(grp):
                        dve.wait_ge(d_dt, 16 * 2)
                    dve.tensor_tensor(dtv[:].rearrange("p (i t) h -> p t i h", t=2),
                                      pf[:, 2, 0:L].rearrange("p (t i n) -> p t i n", t=2, i=GI)[:, :, :, 0:NH],
                                      dtb[:].unsqueeze(1).unsqueeze(1).broadcast_to([P, 2, GI, NH]),
                                      ALU.add).then_inc(dt_dve.sem, 1)
                    dve.wait_ge(dt_dve.sem, dt_dve.at(grp, 1))
                    dve.scalar_tensor_tensor(out=dta[:], in0=dtv[:], scalar=-1.0, in1=dtv[:], op0=ALU.mult,
                                             op1=ALU.max).then_inc(dt_dve.sem, 1)
                elif step == "split2":
                    dve.wait_ge(split[1].sem, split[1].at(grp, 2))
                    later(dve, over, grp, 3)
                    dve.tensor_copy(fst[1][:], pf[:, 1, :]).then_inc(fst_in[1].sem, 1)
                elif step == "conv":
                    conv_and_softplus(grp)
                elif step == "route":
                    route(grp)
                elif step == "route2":
                    route2(grp)
                elif step == "tokens0":
                    tokens(0, 3, grp)
                elif step == "tokens1":
                    tokens(1, 0, grp)
                elif step == "states0":
                    states(0, 3, grp)
                elif step == "states1":
                    states(1, 0, grp)
                elif step == "weights":
                    dve.wait_ge(cw_t.sem, cw_t.at(grp, 1))
                    dve.tensor_copy(cwT[:].rearrange("p q t -> p (q t)"), pf[:, 1, :].bitcast(bf16)).then_inc(cwT_in.sem, 1)
                elif step == "output":
                    dve.wait_ge(o_ps.sem, o_ps.at(grp, 2))
                    c = o_dve
                    mean = pf[:, 0:2, C:C + (TJ - 1) * OW + 1:OW].rearrange("p b j -> p j b")
                    square = pf[:, 0:2, TJ * OW:TJ * OW + TJ].rearrange("p b j -> p j b")
                    dve.tensor_copy(gm[:], mean).then_inc(c.sem, 1)
                    dve.wait_ge(c.sem, c.at(grp, 1))
                    dve.tensor_tensor(gmm[:], gm[:], gm[:], ALU.mult).then_inc(c.sem, 1)
                    dve.wait_ge(c.sem, c.at(grp, 2))
                    dve.tensor_tensor(gv[:], square, gmm[:], ALU.subtract).then_inc(c.sem, 1)
                    dve.wait_ge(c.sem, c.at(grp, 3))
                    dve.tensor_scalar(ge[:], gv[:], 0.0, 1e-5, ALU.max, ALU.add).then_inc(c.sem, 1)
                elif step == "residual":
                    c = o_dve
                    dve.wait_ge(o_pow.sem, o_pow.at(grp, 1))
                    for q in range(2):
                        ins = dve.tensor_tensor(
                            xo[:].rearrange("p (j q) c -> p q j c", q=2)[:, q],
                            pf[:, 1 - q, 0:TJ * OW].rearrange("p (j c) -> p j c", c=OW)[:, :, 0:C],
                            gr[:].rearrange("p (j b) -> p b j", b=2)[:, 1 - q].unsqueeze(2).broadcast_to([P, TJ, C]),
                            ALU.mult)
                    ins.then_inc(c.sem, 1)
                    dve.wait_ge(c.sem, c.at(grp, 5))
                    dve.wait_ge(xpc_in.sem, xpc_in.at(grp, 1))
                    dve.tensor_tensor(x2[:], xo[:], xpc[:], ALU.add).then_inc(c.sem, 1)
                    dve.wait_ge(c.sem, c.at(grp, 6))
                    centre(1, grp, x2[:])

            def back(e, q, grp):
                n = 2 * e + q + 1
                dve.wait_ge(hid_in.sem, hid_in.at(grp, n))
                dve.wait_ge(cwb.sem, cwb.at(grp, n))
                dve.wait_ge(done.sem, done.at(grp, max(e - 1, 0)))
                dve.tensor_tensor(hw[e % 2][:, q, :], hid[:, q, :], pc[:], ALU.mult).then_inc(hw_in.sem, 1)

            def end(grp, nxt):
                if nxt is not None:
                    for q in range(2):
                        if grp is not None:
                            dve.wait_ge(hid_ps.sem, hid_ps.at(grp, 2 * E))
                        dve.wait_ge(fst_in[q].sem, fst_in[q].at(nxt, 1))
                        dve.tensor_copy(bst[q][:], fst[q][:].bitcast(f32)).then_inc(over.sem, 1)
                    if grp is not None:
                        dve.wait_ge(cwb.sem, cwb.at(grp, 2 * E))
                    dve.wait_ge(cwT_in.sem, cwT_in.at(nxt, 1))
                    dve.tensor_copy(bcw[:], cwT[:]).then_inc(over.sem, 1)
                    dve.tensor_copy(bx2[:], x2[:]).then_inc(over.sem, 1)

            run(dve, front, back, end, once)

        @block.tensor
        def _(pe):
            pe.sem_inc(done.sem, 1)
            pe.wait_ge(i_pool, 3)

            def once(step):
                if step == "turn":
                    banks = (ph[0][:], ph[1][:], pc[:], pa[:], pf[:, 0, :])
                    pe.wait_ge(d_wbd, 16)
                    pe.wait_ge(i_dve, 14)
                    for n in range(5):
                        for k in range(4):
                            t, part = 2 * n + k // 2, (taps_h, taps_l)[k % 2]
                            ins = pe.transpose(banks[n][:, P * k:P * k + P], part[:, t].rearrange("p r c -> p (r c)"),
                                               ident[:])
                        ins.then_inc(i_pe, 1)
                    pe.transpose(pf[:, 1, 0:2 * BC], wbd_raw[:].rearrange("o r c -> o (r c)"),
                                 ident[0:2 * BC, 0:2 * BC]).then_inc(i_pe, 1)
                elif step == "z0":
                    pe.wait_ge(i_dve, 20)
                    pe.transpose(pf[:, 0, 0:C], wgc[:], ident[0:C, 0:C])
                    pe.transpose(pf[:, 0, C:2 * C], wo_raw[:], ident[0:C, 0:C])
                    pe.transpose(pf[:, 0, 2 * C:2 * C + E], b1_raw[:], ident[0:E, 0:E]).then_inc(i_pe, 1)
                elif step == "x1":
                    pe.wait_ge(i_dve, 22)
                    pe.wait_ge(i_act, 7)
                    pe.matmul(pa[:, 0:C], lnbB[:], woT[:], start=True, stop=True).then_inc(i_pe, 1)

            def tokens(q, bank, grp):
                pe.wait_ge(zx_up.sem, zx_up.at(grp, 2 * q + 1))
                for j in range(TJ):
                    ins = pe.transpose(pf[:, bank, P * j:P * j + P], xs[:, q, P * j:P * j + P], ident[:])
                ins.then_inc(xs_t.sem, 1)

            def states(q, bank, grp):
                pe.wait_ge(bT_in.sem, bT_in.at(grp, 1))
                pe.wait_ge(v_in.sem, v_in.at(grp, q + 1))
                for t in range(2):
                    for i in (2 * q, 2 * q + 1):
                        ins = pe.matmul(pf[BC * i:BC * i + BC, 2, 0:DI], bT[:, t, i, :],
                                        v[:, q, 2 * (i % 2) + t, :], start=(t == 0), stop=(t == 1))
                ins.then_inc(kv_ps.sem, 1)
                for i in (2 * q, 2 * q + 1):
                    pe.wait_ge(kv_in.sem, kv_in.at(grp, i + 1))
                    ins = pe.matmul(pf[:, bank, L * (i % 2):L * (i % 2) + L], kv[:, i, :], bc[:],
                                    start=True, stop=True)
                ins.then_inc(y_ps.sem, 1)

            def project_x(q, bank, grp):
                for t in range(TAPS):
                    for s in range(2):
                        ins = pe.matmul(bank, wT[:, t, s, :],
                                        pad[q][:, :, t // 3:t // 3 + HH, t % 3:t % 3 + WW],
                                        start=(t == 0 and s == 0), stop=(t == TAPS - 1 and s == 1))
                ins.then_inc(zx.sem, 1)

            def project_z(q, bank, grp):
                for s in range(2):
                    ins = pe.matmul(bank, wT[:, TAPS, s, :], interior(pad[q]), start=(s == 0), stop=(s == 1))
                ins.then_inc(zx.sem, 1)

            def parts(n, bank, grp):
                pe.wait_ge(ln_dve[n].sem, ln_dve[n].at(grp, 6))
                for q in range(2):
                    for j in range(TJ):
                        ins = pe.transpose(pf[:, bank + q, P * j:P * j + P],
                                           ln[n]["hl"][:, 2 * j + q].rearrange("p r c -> p (r c)"), ident[:])
                    ins.then_inc(split[n].sem, 1)

            def front(step, grp):
                if step == "turn":
                    pe.wait_ge(x_in.sem, x_in.at(grp, 32))
                    later(pe, kv_in, grp, GI)
                    for j in range(TJ):
                        ins = pe.transpose(pf[:, 2, P * j:P * j + P], xin[:, P * j:P * j + P], ident[:])
                    ins.then_inc(turned.sem, 1)
                elif step == "split1":
                    pe.wait_ge(kept.sem, kept.at(grp, 1))
                    later(pe, y_dve, grp, 1)
                    parts(0, 2, grp)
                elif step == "split2":
                    pe.wait_ge(o_dve.sem, o_dve.at(grp, 5))
                    parts(1, 0, grp)
                elif step == "bd":
                    pe.wait_ge(padded[0].sem, padded[0].at(grp, 1))
                    pe.wait_ge(padded[1].sem, padded[1].at(grp, 1))
                    if first(grp):
                        pe.wait_ge(i_act, 3)
                        pe.wait_ge(i_dve, 17)
                    for part in range(2):
                        for i in range(GI):
                            ins = pe.matmul(pf[BC * i:BC * i + BC, 2, L * part:L * part + L],
                                            wbd[:, BC * part:BC * part + BC],
                                            interior(pad[i // 2])[:, i % 2].bitcast(f32), start=True, stop=True)
                    ins.then_inc(bd.sem, 1)
                    pe.wait_ge(dtc_in.sem, dtc_in.at(grp, 1))
                    pe.wait_ge(bcp_in.sem, bcp_in.at(grp, 1))
                    for t in range(2):
                        ins = pe.transpose(pf[:, 2, P * t:P * t + P], dtc[:, P * t:P * t + P], ident[:])
                    ins.then_inc(dt_t.sem, 1)
                elif step == "x0":
                    if not isinstance(grp, int):
                        pe.wait_ge(hw_in.sem, hw_in.at(grp - 2, BREAK))
                    if first(grp):
                        pe.wait_ge(i_dve, 17)
                    project_x(0, ph[0][:], grp)
                elif step == "z0":
                    pe.wait_ge(dt_dve.sem, dt_dve.at(grp, 1))
                    project_z(0, pf[:, 2, :], grp)
                elif step == "tokens0":
                    pe.wait_ge(bc_in.sem, bc_in.at(grp, 1))
                    pe.wait_ge(zx_up.sem, zx_up.at(grp, 2))
                    for t in range(2):
                        ins = pe.transpose(pf[:, 2, P * t:P * t + P], bc[:, P * t:P * t + P], ident[:])
                    ins.then_inc(bT_t.sem, 1)
                    tokens(0, 3, grp)
                elif step == "x1":
                    project_x(1, ph[1][:], grp)
                elif step == "z1":
                    project_z(1, pc[:], grp)
                elif step == "states0":
                    states(0, 3, grp)
                elif step == "tokens1":
                    later(pe, fst_in[0], grp, 1)
                    tokens(1, 0, grp)
                    pe.wait_ge(zx_up.sem, zx_up.at(grp, 4))
                elif step == "states1":
                    states(1, 0, grp)
                elif step == "output":
                    if first(grp):
                        pe.wait_ge(i_act, ACT_ALL)
                        pe.wait_ge(i_pool, POOL_ALL)
                    later(pe, cwT_in, grp, 1)
                    for q in range(2):
                        pe.wait_ge(y_dve.sem, y_dve.at(grp, 2 * q + 2))
                        pe.wait_ge(gsq_in.sem, gsq_in.at(grp, q + 1))
                        for j in range(TJ):
                            pe.matmul(pf[:, 1 - q, OW * j:OW * j + OW], g[:, q, P * j:P * j + P], wo[:],
                                      start=True, stop=True)
                            ins = pe.matmul(pf[:, 1 - q, TJ * OW + j:TJ * OW + j + 1], gsq[:, q, P * j:P * j + P],
                                            ones[:], start=True, stop=True)
                        ins.then_inc(o_ps.sem, 1)
                elif step == "gate":
                    pe.wait_ge(fst_in[0].sem, fst_in[0].at(grp, 1))
                    pe.wait_ge(fst_in[1].sem, fst_in[1].at(grp, 1))
                    for j in range(TJ):
                        for q in range(2):
                            n = 2 * j + q
                            ins = pe.matmul(pf[:, 1, E * n:E * n + E], fst[q][:, P * j:P * j + P].bitcast(f32), gw[:],
                                            start=True, stop=True)
                    ins.then_inc(gate_ps.sem, 1)
                elif step == "weights":
                    pe.wait_ge(rt.sem, rt.at(grp, rt.per))
                    for q in range(2):
                        for j in range(TJ):
                            ins = pe.transpose(pf[:, 1, :].bitcast(bf16)[:, HT * q + P * j:HT * q + P * j + P],
                                               cwp[:, 2 * j + q, :], identb[:])
                    ins.then_inc(cw_t.sem, 1)

            def open_output(grp):
                pe.wait_ge(over.sem, over.at(grp, 4))
                pe.wait_ge(ost_in.sem, ost_in.at(grp, 0))
                for s in range(PARTS):
                    for q in range(2):
                        pe.matmul(pa[C * q:C * q + C, :], b2p[:, s, :], bcw[:, q, :], start=(s == 0), stop=False)
                for j in range(TJ):
                    for q in range(2):
                        pe.matmul(pa[C * q:C * q + C, P * j:P * j + P], bx2[:, 2 * j + q, :], ident[:],
                                  start=False, stop=False)

            def add(e, grp):
                for q in range(2):
                    pe.wait_ge(hw_in.sem, hw_in.at(grp, 2 * e + q + 1))
                for q in range(2):
                    ins = pe.matmul(pa[C * q:C * q + C, :], w2[:, e, :], hw[e % 2][:, q, :], start=False,
                                    stop=(e == E - 1))
                ins.then_inc(done.sem, 1)

            def back(e, q, grp):
                n = 2 * e + q
                if n == 0:
                    pe.wait_ge(over.sem, over.at(grp, 3))
                pe.wait_ge(hid_in.sem, hid_in.at(grp, max(n - 1, 0)))
                pe.matmul(ph[q][:], w1h[:, e, :], bst[q][:], start=True, stop=False)
                pe.matmul(ph[q][:], w1l[:, e, :], bst[q][:], start=False, stop=True).then_inc(hid_ps.sem, 1)
                if q == 1 and e > 0:
                    add(e - 1, grp)
                pe.wait_ge(hw_in.sem, hw_in.at(grp, n))
                pe.matmul(pc[:], sel[:, e, :], bcw[:, q, :], start=True, stop=True).then_inc(cwb.sem, 1)
                if n == 0:
                    open_output(grp)
                if n == 2 * E - 1:
                    add(e, grp)

            def end(grp, nxt):
                if grp is None:
                    pe.wait_ge(i_dve, 31)
                    pe.wait_ge(i_act, ACT_ALL)

            run(pe, front, back, end, once)


_INS = ["x", "L0_conv_W_in", "L0_conv_conv_w", "L0_conv_conv_b", "L0_conv_dt_bias", "L0_conv_A_log", "L0_conv_D",
        "L0_conv_ln_g", "L0_conv_ln_b", "L0_conv_W_out", "L0_ffn_gate_w", "L0_ffn_gate_b", "L0_ffn_W1", "L0_ffn_b1",
        "L0_ffn_W2", "L0_ffn_b2"]


def kernel(**inputs):
    import numpy as _np
    import concourse.bacc as _bacc
    from concourse import mybir as _mybir
    from concourse.bass_utils import run_bass_kernel_spmd as _run

    nc = _bacc.Bacc("TRN2", target_bir_lowering=False, num_devices=1)
    arrays, args = {}, []
    for name in _INS:
        a = _np.ascontiguousarray(inputs[name])
        arrays[f"in_{name}_dram"] = a
        args.append(nc.dram_tensor(f"in_{name}_dram", a.shape, _mybir.dt.from_np(a.dtype), kind="ExternalInput").ap())
    shape = inputs["x"].shape
    out = nc.dram_tensor("out_0_dram", shape, _mybir.dt.float32, kind="ExternalOutput").ap()
    metaformer_block(nc, *args, out)
    r = _run(nc, [arrays], core_ids=[0])
    return r.results[0]["out_0_dram"]
```

```python
import concourse.bass as bass
from concourse import mybir
from contextlib import ExitStack


class Count:

    def __init__(self, sem, per, base=0):
        self.sem, self.per, self.base = sem, per, base

    def at(self, g, k):
        return g * self.per + k + self.base


def metaformer_block(nc, x, W_in, conv_w, conv_b, dt_bias, A_log, D, ln_g, ln_b, W_out,
                     gate_w, gate_b, W1, b1, W2, b2, out):
    f32, f32r, bf16 = mybir.dt.float32, mybir.dt.float32r, mybir.dt.bfloat16
    ALU, ACT, AX = mybir.AluOpType, mybir.ActivationFunctionType, mybir.AxisListType

    B, C, HH, WW = x.shape
    DI = W_out.shape[1]
    NH = A_log.shape[0]
    HD = DI // NH
    NS = (conv_w.shape[0] - DI) // 2
    E, _, F = W1.shape
    L = HH * WW
    GI = 4
    NG = B // GI
    P = 128
    HT = 2 * L
    TJ = HT // P
    NT = 2 * TJ
    TAPS = 9
    PH, PW = HH + 2, WW + 2
    BC = 2 * NS
    OW = C + 1
    PARTS = 3

    x_v = x.rearrange("(g q b) c h w -> g q c b (h w)", q=2, b=2)
    out_v = out.rearrange("(g q b) c h w -> g q c b (h w)", q=2, b=2)
    cw_v = conv_w.rearrange("o a kh kw -> o (a kh kw)")

    def column(v):
        return v.rearrange("(n a) -> n a", a=1)

    def rows(v, n):
        return v.rearrange("(a n) -> a n", a=1).broadcast_to([n, v.shape[0]])

    ctx = ExitStack()
    with ctx:
        def sb(name, shape, dt=f32):
            return ctx.enter_context(nc.sbuf_tensor(name, shape, dt))

        def sem(name):
            return ctx.enter_context(nc.semaphore(name))

        def count(name, per, base=0):
            return Count(sem(name), per, base)

        ident = sb("ident", [P, P])
        identb = sb("identb", [P, P], bf16)
        identr = sb("identr", [P, 3 * P], f32r)
        centring = sb("centring", [P, P])
        wx_raw = sb("wx_raw", [P, C])
        wz_raw = sb("wz_raw", [P, C])
        wbd_raw = sb("wbd_raw", [2 * BC, 2, C])
        cw_x = sb("cw_x", [P, TAPS])
        cb_x = sb("cb_x", [P, 1])
        cw_bc = sb("cw_bc", [P, TAPS])
        cb_bc = sb("cb_bc", [P, 1])
        wo_raw = sb("wo_raw", [C, DI])
        lng = sb("lng", [C, DI])
        lnb = sb("lnb", [DI, 1])
        dskip = sb("dskip", [DI, 1])
        dtb = sb("dtb", [P, NH])
        alog = sb("alog", [P, NH])
        w1_raw = sb("w1_raw", [P, E, F])
        w2 = sb("w2", [F, E, C])
        b1_raw = sb("b1_raw", [E, F])
        b2_raw = sb("b2_raw", [PARTS * E, C])
        gw = sb("gw", [P, E])
        gb = sb("gb", [P, E])
        tapw = sb("tapw", [P, TAPS + 1, C])
        taps_h = sb("taps_h", [P, TAPS + 1, 2, C], f32r)
        taps_l = sb("taps_l", [P, TAPS + 1, 2, C], f32r)
        wT = sb("wT", [P, 5, 2, 2, DI], f32r)
        wbd = sb("wbd", [P, 2 * BC])
        wg = sb("wg", [C, DI])
        wgs = sb("wgs", [C, 1])
        wgc = sb("wgc", [C, DI])
        wo = sb("wo", [DI, OW])
        woT = sb("woT", [DI, C])
        lnbB = sb("lnbB", [DI, P])
        c0 = sb("c0", [P, C])
        expA = sb("expA", [P, NH])
        w1h = sb("w1h", [P, E, F], f32r)
        w1l = sb("w1l", [P, E, F], f32r)
        b1T = sb("b1T", [F, E])
        b2p = sb("b2p", [P, PARTS, C], bf16)
        b2f = sb("b2f", [PARTS * E, 2, C])
        selc = sb("selc", [P, 2, E])
        sel = sb("sel", [P, E, P], bf16)
        rank = sb("rank", [P, E])
        halves = sb("halves", [P, NT])
        xin = sb("xin", [P, HT])
        xtok = sb("xtok", [P, NT, C])
        xpc = sb("xpc", [P, NT, C])
        ln = []
        for n in (1, 2):
            ln.append(dict(
                sq=sb(f"ln{n}_sq", [P, NT, C]),
                s2=sb(f"ln{n}_s2", [P, NT]), ve=sb(f"ln{n}_ve", [P, NT]), r=sb(f"ln{n}_r", [P, NT]),
                xn=sb(f"ln{n}_xn", [P, NT, C]), hl=sb(f"ln{n}_hl", [P, NT, 2, C], f32r)))
        ln[1].update(s1=sb("ln2_s1", [P, NT]), xc=sb("ln2_xc", [P, NT, C]))
        pad = [sb(f"pad{q}", [P, 2, PH, PW], f32r) for q in range(2)]
        sz = sb("sz", [P, 2, HT])
        xs = sb("xs", [P, 2, HT])
        bcp = sb("bcp", [P, PH, PW])
        bcc = sb("bcc", [P, HH, WW])
        bc = sb("bc", [P, L])
        dtc = sb("dtc", [P, L])
        dtv = sb("dtv", [P, GI * 2, NH])
        dta = sb("dta", [P, GI * 2, NH])
        dtu = sb("dtu", [P, GI * 2, NH])
        dtd = sb("dtd", [P, GI * 2, NH])
        dts = sb("dts", [P, GI * 2, NH])
        dtq = sb("dtq", [P, GI * 2, NH])
        dtp = sb("dtp", [P, GI * 2, NH])
        dA = sb("dA", [P, GI * 2, NH])
        bT = sb("bT", [P, 2, GI, BC])
        v = sb("v", [P, 2, TJ, DI])
        kv = sb("kv", [P, GI, DI])
        gy = sb("gy", [P, 2, HT])
        g = sb("g", [P, 2, HT])
        gsq = sb("gsq", [P, 2, HT])
        gm = sb("gm", [P, TJ, 2])
        gmm = sb("gmm", [P, TJ, 2])
        gv = sb("gv", [P, TJ, 2])
        ge = sb("ge", [P, TJ, 2])
        gr = sb("gr", [P, NT])
        xo = sb("xo", [P, NT, C])
        x2 = sb("x2", [P, NT, C])
        fst = [sb(f"fst{q}", [P, HT], f32r) for q in range(2)]
        ones = sb("ones", [P, 1])
        lg = sb("lg", [P, NT, E])
        m1 = sb("m1", [P, NT])
        ld = sb("ld", [P, NT, E])
        th = sb("th", [P, NT, E])
        tn = sb("tn", [P, NT, E])
        td = sb("td", [P, NT, E])
        pe_ = sb("pe_", [P, NT, E])
        ps_ = sb("ps_", [P, NT])
        pr = sb("pr", [P, NT])
        k1 = sb("k1", [P, NT, E])
        kk = sb("kk", [P, NT])
        o1 = sb("o1", [P, NT, E])
        lg2 = sb("lg2", [P, NT, E])
        o2 = sb("o2", [P, NT, E])
        cw = sb("cw", [P, NT, E])
        cr = sb("cr", [P, 2, NT, E])
        cwp = sb("cwp", [P, NT, P], bf16)
        cwT = sb("cwT", [P, 2, HT], bf16)
        bst = [sb(f"bst{q}", [P, HT], f32r) for q in range(2)]
        bcw = sb("bcw", [P, 2, HT], bf16)
        hid = [sb(f"hid{k}", [P, 2, HT]) for k in range(2)]
        hw = [sb(f"hw{k}", [P, 2, HT]) for k in range(2)]
        ost = sb("ost", [P, HT])

        pf = ctx.enter_context(nc.psum_tensor("pf", [P, 4, HT], f32))
        ph = [ctx.enter_context(nc.psum_tensor(f"ph{q}", [P, HT], f32)) for q in range(2)]
        pc = ctx.enter_context(nc.psum_tensor("pc", [P, HT], f32))
        pa = ctx.enter_context(nc.psum_tensor("pa", [P, HT], f32))

        d_proj = sem("d_proj")
        d_bc = sem("d_bc")
        d_mix = sem("d_mix")
        d_exp = sem("d_exp")
        d_wbd = sem("d_wbd")
        d_dt = sem("d_dt")
        MIX, CONV, EXP = 5, 1 + 2 * GI, 6 + PARTS
        POOL_ALL, ACT_ALL = 19 + E, 9
        i_pool = sem("i_pool")
        i_dve = sem("i_dve")
        i_pe = sem("i_pe")
        i_act = sem("i_act")
        x_in = count("x_in", 32)
        x_out = count("x_out", 32, 1)
        turned = count("turned", 2)
        kept = count("kept", 1)
        xpc_in = count("xpc_in", 1)
        CENTRE = (0, 2)
        ln_dve = [count(f"ln{n + 1}_dve", CENTRE[n] + 4) for n in (0, 1)]
        ln_sq = [count(f"ln{n}_sqd", 1) for n in (1, 2)]
        ln_pow = [count(f"ln{n}_pow", 1) for n in (1, 2)]
        ln_high = [count(f"ln{n}_high", 1) for n in (1, 2)]
        split = [count(f"split{n}", 2) for n in (1, 2)]
        padded = [count(f"padded{q}", 1) for q in range(2)]
        bd = count("bd", 1)
        bcp_in = count("bcp_in", 1)
        dtc_in = count("dtc_in", 1)
        dt_t = count("dt_t", 1)
        dt_dve = count("dt_dve", 16)
        dt_exp = count("dt_exp", 1)
        bc_conv = count("bc_conv", TAPS)
        bc_in = count("bc_in", 1)
        zx = count("zx", 4)
        zx_up = count("zx_up", 4)
        bT_t = count("bT_t", 1)
        bT_in = count("bT_in", 1)
        xs_t = count("xs_t", 2)
        v_in = count("v_in", 2)
        kv_ps = count("kv_ps", 1)
        kv_in = count("kv_in", GI)
        y_ps = count("y_ps", 2)
        y_dve = count("y_dve", 4)
        gsq_in = count("gsq_in", 2)
        o_ps = count("o_ps", 2)
        o_dve = count("o_dve", 6)
        o_pow = count("o_pow", 1)
        fst_in = [count(f"fst_in{q}", 1) for q in range(2)]
        gate_ps = count("gate_ps", 1)
        rt = count("rt", 25)
        rt_tanh = count("rt_tanh", 1)
        cw_t = count("cw_t", 1)
        cwT_in = count("cwT_in", 1)
        bst_in = count("bst_in", 2)
        bcw_in = count("bcw_in", 1)
        opened = count("opened", 1)
        hid_ps = count("hid_ps", 2 * E)
        hid_in = count("hid_in", 2 * E, 1)
        cwb = count("cwb", 2 * E)
        hw_in = count("hw_in", 2 * E, 1)
        done = count("done", E, 1)
        ost_in = count("ost_in", 1, 1)

        PLAN = [("router", "residual"), ("mixer", "turn"), ("back", 0), ("back", 1), ("mixer", "keep"),
                ("mixer", "var1"), ("back", 2), ("router", "sum"), ("back", 3), ("back", 4), ("mixer", "norm1"),
                ("router", "centre2"), ("mixer", "low1"), ("back", 5), ("mixer", "split1"), ("router", "var2"),
                ("back", 6), ("mixer", "bd"), ("back", 7), ("router", "norm2"), ("mixer", "bdt"),
                ("mixer", "x0a"), ("router", "low2"), ("back", 8), ("router", "split2"), ("mixer", "conv0"),
                ("mixer", "x0b"), ("mixer", "conv1"), ("router", "gate"), ("back", 9), ("router", "route"),
                ("back", 10), ("mixer", "x0c"), ("mixer", "conv2"), ("router", "route1"), ("mixer", "x1a"),
                ("back", 11), ("router", "route2"), ("mixer", "x1b"), ("back", 12), ("mixer", "x1c"),
                ("mixer", "xpc"), ("router", "weights"), ("mixer", "z"), ("mixer", "soft0"), ("mixer", "soft1"),
                ("mixer", "tokens0"), ("mixer", "tokens1"), ("back", 13), ("mixer", "states0"),
                ("mixer", "states1"), ("mixer", "output0"), ("back", 14), ("back", 15), ("mixer", "output1")]

        BUSY = {"norm1": 2, "low1": 2, "centre2": 4, "var2": 3, "norm2": 3, "low2": 2, "route": 2, "z": 4,
                "busy0": 3, "busy1": 5, "busy2": 1, "busy3": 5, "busy4": 2, "busy5": 5}

        PROLOGUE = [("mixer", "turn"), ("mixer", "keep"), ("mixer", "var1"), ("setup", "tapsa"),
                    ("setup", "tapsb"), ("mixer", "norm1"), ("setup", "low"), ("mixer", "low1"),
                    ("setup", "taps_in"), ("mixer", "split1"), ("mixer", "bd"), ("setup", "busy0"),
                    ("mixer", "bdt"), ("setup", "alog"), ("mixer", "conv0"), ("mixer", "conv1"),
                    ("mixer", "conv2"), ("mixer", "x0a"), ("mixer", "x0b"), ("setup", "norm"), ("setup", "busy1"),
                    ("setup", "norm_t"), ("setup", "c0"), ("mixer", "x0c"), ("mixer", "xpc"), ("mixer", "x1a"),
                    ("mixer1", "turn"), ("mixer1", "keep"), ("mixer", "x1b"), ("mixer", "x1c"),
                    ("mixer1", "var1"), ("mixer", "z"), ("mixer", "soft0"), ("mixer", "soft1"),
                    ("mixer1", "norm1"), ("mixer", "tokens0"), ("mixer", "tokens1"), ("setup", "experts"),
                    ("mixer1", "low1"), ("mixer", "states0"), ("mixer", "states1"), ("setup", "busy2"),
                    ("mixer1", "split1"), ("setup", "busy3"), ("mixer", "output0"), ("mixer", "output1"),
                    ("mixer1", "bd"), ("router", "residual"), ("router", "sum"), ("router", "centre2"),
                    ("setup", "busy4"), ("router", "var2"), ("mixer1", "bdt"), ("mixer1", "x0a"),
                    ("mixer1", "conv0"), ("mixer1", "x0b"), ("mixer1", "x0c"), ("router", "norm2"),
                    ("mixer1", "conv1"), ("router", "low2"), ("router", "split2"), ("router", "gate"),
                    ("mixer1", "x1a"), ("mixer1", "conv2"), ("mixer1", "x1b"), ("router", "route"),
                    ("mixer1", "x1c"), ("setup", "busy5"), ("router", "route1"), ("mixer1", "z"),
                    ("mixer1", "xpc"), ("mixer1", "soft0"), ("router", "route2"), ("mixer1", "soft1"),
                    ("mixer1", "tokens0"), ("mixer1", "tokens1"), ("router", "weights"), ("mixer1", "states0"),
                    ("mixer1", "states1"), ("mixer1", "output0"), ("mixer1", "output1")]

        EPILOGUE = [("back", 0), ("back", 1), ("router", "residual"), ("back", 2), ("router", "sum"),
                    ("back", 3), ("router", "centre2"), ("back", 4), ("router", "var2"), ("back", 5), ("back", 6),
                    ("router", "norm2"), ("router", "low2"), ("back", 7), ("back", 8), ("router", "split2"),
                    ("back", 9), ("router", "gate"), ("router", "route"), ("back", 10), ("router", "route1"),
                    ("back", 11), ("router", "route2"), ("back", 12), ("back", 13), ("router", "weights"),
                    ("back", 14), ("back", 15)]

        def run(eng, front, back, end, setup=lambda step: None):
            for part, step in PROLOGUE:
                if part == "setup":
                    setup(step)
                else:
                    front(step, 1 if part == "mixer1" else 0)
            end(None, 0)
            with eng.Fori(0, NG - 2) as i:
                for part, step in PLAN:
                    if part == "back":
                        back(step // 2, step % 2, i)
                    else:
                        front(step, i + 1 if part == "router" else i + 2)
                end(i, i + 1)
            for part, step in EPILOGUE:
                if part == "back":
                    back(step // 2, step % 2, NG - 2)
                else:
                    front(step, NG - 1)
            end(NG - 2, NG - 1)
            for u in range(2 * E):
                back(u // 2, u % 2, NG - 1)
            end(NG - 1, None)

        def mixer_bank(k, grp):
            return ph[k][:] if isinstance(grp, int) and grp == 1 else pf[:, 2 + k, :]

        def later(eng, c, grp, k):
            if not (isinstance(grp, int) and grp == 0):
                eng.wait_ge(c.sem, c.at(grp - 1, k))

        def first(grp):
            return isinstance(grp, int) and grp == 0

        def interior(t):
            return t[:, :, 1:1 + HH, 1:1 + WW]

        block = ctx.enter_context(nc.Block())

        @block.sync
        def _(sp):
            sp.sem_inc(x_out.sem, 1)

            def load(grp):
                later(sp, turned, grp, 2)
                for q in range(2):
                    sp.dma_start(xin[C * q:C * q + C, :].rearrange("c (b l) -> c b l", b=2),
                                 x_v[grp, q]).then_inc(x_in.sem, 16)

            load(0)
            sp.dma_start(wx_raw[:], W_in[DI:2 * DI, :]).then_inc(d_proj, 16)
            sp.dma_start(cw_x[:], cw_v[0:DI, :]).then_inc(d_proj, 16)
            sp.dma_start(wz_raw[:], W_in[0:DI, :]).then_inc(d_proj, 16)
            sp.wait_ge(i_pool, 1)
            sp.dma_start(wbd_raw[0:BC + NH, :, :],
                         W_in[2 * DI:2 * DI + BC + NH, :].unsqueeze(1).broadcast_to([BC + NH, 2, C])).then_inc(d_wbd, 16)
            sp.dma_start(dtb[:], rows(dt_bias, P)).then_inc(d_dt, 16)
            sp.dma_start(alog[:], rows(A_log, P)).then_inc(d_dt, 16)
            for i in range(GI):
                sp.dma_start(cw_bc[BC * i:BC * i + BC, :], cw_v[DI:DI + BC, :]).then_inc(d_bc, 16)
            for i in range(GI):
                sp.dma_start(cb_bc[BC * i:BC * i + BC, :], column(conv_b)[DI:DI + BC, :]).then_inc(d_bc, 16)
            sp.dma_start(cb_x[:], column(conv_b)[0:DI, :]).then_inc(d_bc, 16)
            sp.dma_start(wo_raw[:], W_out).then_inc(d_mix, 16)
            sp.dma_start(lng[:], rows(ln_g, C)).then_inc(d_mix, 16)
            sp.dma_start(lnb[:], column(ln_b)).then_inc(d_mix, 16)
            sp.dma_start(dskip[:], column(D).unsqueeze(1).broadcast_to([NH, HD, 1])).then_inc(d_mix, 16)
            sp.dma_start(b1_raw[:], b1).then_inc(d_mix, 16)
            load(1)
            sp.dma_start(gb[:], rows(gate_b, P)).then_inc(d_exp, 16)
            for r in range(2):
                sp.dma_start(gw[C * r:C * r + C, :], gate_w).then_inc(d_exp, 16)
            for r in range(2):
                sp.dma_start(w1_raw[C * r:C * r + C, :, :], W1.rearrange("e c f -> c e f")).then_inc(d_exp, 16)
            for r in range(PARTS):
                sp.dma_start(b2_raw[E * r:E * r + E, :], b2).then_inc(d_exp, 16)
            sp.dma_start(w2[:], W2.rearrange("e f c -> f e c")).then_inc(d_exp, 16)

            with sp.Fori(0, NG - 2) as i:
                load(i + 2)
            sp.wait_ge(x_out.sem, x_out.at(NG - 1, 32))

        @block.gpsimd
        def _(pool):
            pool.memset(wbd_raw[:], 0.0).then_inc(i_pool, 1)
            pool.memset(ident[:], 0.0).then_inc(i_pool, 1)
            pool.wait_ge(i_pool, 2)
            pool.affine_select(out=ident[:], in_=ident[:], compare_op=ALU.not_equal, fill=1.0, base=0,
                               pattern=[[-1, P]], channel_multiplier=1).then_inc(i_pool, 1)
            pool.memset(halves[:], -0.5).then_inc(i_pool, 1)
            pool.memset(centring[:], 0.0).then_inc(i_pool, 1)
            pool.wait_ge(i_pool, 5)
            for r in range(P // C):
                pool.memset(centring[C * r:C * r + C, C * r:C * r + C], -1.0 / C).then_inc(i_pool, 1)
            pool.wait_ge(i_pool, 7)
            pool.tensor_tensor(centring[:], centring[:], ident[:], ALU.add).then_inc(i_pool, 1)
            pool.memset(identr[:].bitcast(f32), 0.0).then_inc(i_pool, 1)
            pool.wait_ge(i_pool, 9)
            pool.tensor_copy(identr[:, P:2 * P], ident[:]).then_inc(i_pool, 1)
            pool.memset(pad[0][:].bitcast(f32), 0.0).then_inc(i_pool, 1)
            pool.memset(pad[1][:].bitcast(f32), 0.0).then_inc(i_pool, 1)
            pool.memset(bcp[:], 0.0).then_inc(i_pool, 1)
            pool.memset(bT[:], 0.0).then_inc(i_pool, 1)
            pool.memset(kv[:], 0.0).then_inc(i_pool, 1)
            def setup(step):
                if step == "low":
                    pool.memset(cwp[:], 0.0).then_inc(i_pool, 1)
                    pool.memset(b2p[:], 0.0).then_inc(i_pool, 1)
                    pool.memset(ones[:], 1.0 / DI).then_inc(i_pool, 1)
                    for e in range(E):
                        pool.memset(rank[:, e:e + 1], float(E - e)).then_inc(i_pool, 1)
                    pool.tensor_copy(identb[:], ident[:]).then_inc(i_pool, 1)

            def power(n, grp):
                pool.wait_ge(ln_dve[n].sem, ln_dve[n].at(grp, CENTRE[n] + 2))
                pool.tensor_tensor(ln[n]["r"][:], ln[n]["ve"][:], halves[:], ALU.pow).then_inc(ln_pow[n].sem, 1)

            def front(step, grp):
                if step == "var1":
                    power(0, grp)
                elif step == "var2":
                    power(1, grp)
                elif step == "xpc":
                    pool.wait_ge(kept.sem, kept.at(grp, 1))
                    if first(grp):
                        pool.wait_ge(i_act, ACT_ALL - 1)
                    later(pool, o_dve, grp, 6)
                    pool.tensor_tensor(xpc[:], xtok[:], c0[:].unsqueeze(1).broadcast_to([P, NT, C]),
                                       ALU.add).then_inc(xpc_in.sem, 1)
                elif step == "output1":
                    pool.wait_ge(o_dve.sem, o_dve.at(grp, 4))
                    pool.tensor_tensor(gr[:], ge[:].rearrange("p j q -> p (j q)"), halves[:],
                                       ALU.pow).then_inc(o_pow.sem, 1)

            run(pool, front, lambda e, q, grp: None, lambda grp, nxt: None, setup)

        @block.scalar
        def _(act):
            act.sem_inc(hid_in.sem, 1)
            act.sem_inc(ost_in.sem, 1)

            def setup(step):
                if step == "taps_in":
                    for n, bank in ((1, ph[1]), (3, pa)):
                        act.wait_ge(i_pe, n + 1)
                        act.activation(wT[:, n].rearrange("p s t o -> p (s t o)"), bank[:],
                                       ACT.Copy).then_inc(i_act, 1)
                    act.wait_ge(i_pe, 6)
                    act.activation(wbd[:], pf[:, 1, 0:2 * BC], ACT.Copy).then_inc(i_act, 1)
                elif step == "alog":
                    act.wait_ge(d_dt, 16 * 2)
                    act.activation(expA[:], alog[:], ACT.Exp).then_inc(i_act, 1)
                elif step == "norm_t":
                    act.wait_ge(i_pe, 7)
                    act.activation(wo[:, 0:C], pf[:, 0, 0:C], ACT.Copy).then_inc(i_act, 1)
                    act.activation(woT[:], pf[:, 0, C:2 * C], ACT.Copy).then_inc(i_act, 1)
                    act.activation(b1T[:], pf[:, 0, 2 * C:2 * C + E], ACT.Copy).then_inc(i_act, 1)
                elif step == "c0":
                    act.wait_ge(i_pe, 8)
                    act.activation(c0[:], pa[:, 0:C], ACT.Copy).then_inc(i_act, 1)
                elif step == "experts":
                    act.wait_ge(d_exp, 16 * EXP)
                    act.activation(w1h[:], w1_raw[:], ACT.Copy).then_inc(i_act, 1)


            def high(n, grp):
                act.wait_ge(ln_dve[n].sem, ln_dve[n].at(grp, CENTRE[n] + 3))
                later(act, split[n], grp, 2)
                act.activation(ln[n]["hl"][:, :, 0, :], ln[n]["xn"][:], ACT.Copy)\
                   .then_inc(ln_high[n].sem, 1)

            def silu(k, out_, bank, bias, grp):
                act.wait_ge(zx.sem, zx.at(grp, k))
                later(act, y_dve, grp, 4)
                if k == 1 and first(grp):
                    act.wait_ge(d_bc, 16 * CONV)
                act.activation(out_, bank, ACT.Silu, bias=bias).then_inc(zx_up.sem, 1)

            def states(q, grp):
                act.wait_ge(kv_ps.sem, kv_ps.at(grp, 1))
                later(act, y_ps, grp, 2)
                for i in (2 * q, 2 * q + 1):
                    rws = slice(BC * i, BC * i + BC)
                    act.activation(kv[rws, i, :], mixer_bank(0, grp)[rws, 0:DI], ACT.Copy).then_inc(kv_in.sem, 1)

            def gated(q, grp):
                act.wait_ge(y_dve.sem, y_dve.at(grp, 2 * q + 2))
                later(act, o_ps, grp, 2)
                act.activation(gsq[:, q, :], g[:, q, :], ACT.Square).then_inc(gsq_in.sem, 1)

            def front(step, grp):
                if step == "keep":
                    act.wait_ge(turned.sem, turned.at(grp, 1))
                    later(act, ln_dve[0], grp, 1)
                    act.activation(ln[0]["sq"][:].rearrange("p t c -> p (t c)"), mixer_bank(0, grp),
                                   ACT.Square).then_inc(ln_sq[0].sem, 1)
                    act.wait_ge(turned.sem, turned.at(grp, 2))
                    later(act, xpc_in, grp, 1)
                    act.activation(xtok[:].rearrange("p t c -> p (t c)"), mixer_bank(1, grp), ACT.Copy).then_inc(kept.sem, 1)
                elif step == "centre2":
                    act.wait_ge(ln_dve[1].sem, ln_dve[1].at(grp, 2))
                    act.activation(ln[1]["sq"][:], ln[1]["xc"][:], ACT.Square).then_inc(ln_sq[1].sem, 1)
                elif step == "norm1":
                    high(0, grp)
                elif step == "norm2":
                    high(1, grp)
                elif step == "split1":
                    act.wait_ge(split[0].sem, split[0].at(grp, 1))
                    if first(grp):
                        act.wait_ge(i_pool, 15)
                    later(act, zx, grp, 4)
                    act.activation(interior(pad[0]), mixer_bank(0, grp).rearrange("p (b h w) -> p b h w", b=2, h=HH),
                                   ACT.Copy).then_inc(padded[0].sem, 1)
                elif step == "z":
                    act.wait_ge(dt_dve.sem, dt_dve.at(grp, 2))
                    act.activation(dtu[:], dta[:], ACT.Exp, scale=-1.0).then_inc(dt_exp.sem, 1)
                    silu(1, xs[:, 0, :], mixer_bank(1, grp), cb_x[:, 0:1], grp)
                    silu(2, xs[:, 1, :], mixer_bank(0, grp), cb_x[:, 0:1], grp)
                    act.wait_ge(bc_conv.sem, bc_conv.at(grp, TAPS))
                    later(act, y_ps, grp, 2)
                    act.activation(bc[:], bcc[:].rearrange("p h w -> p (h w)"), ACT.Silu,
                                   bias=cb_bc[:, 0:1]).then_inc(bc_in.sem, 1)
                    silu(3, sz[:, 0, :], mixer_bank(1, grp), 0.0, grp)
                    silu(4, sz[:, 1, :], mixer_bank(0, grp), 0.0, grp)
                elif step == "split2":
                    act.wait_ge(split[1].sem, split[1].at(grp, 1))
                    later(act, bst_in, grp, 1)
                    act.activation(fst[0][:], pf[:, 0, :], ACT.Copy).then_inc(fst_in[0].sem, 1)
                elif step == "route":
                    act.wait_ge(rt.sem, rt.at(grp, 3))
                    act.activation(th[:], ld[:], ACT.Tanh, scale=0.5).then_inc(rt_tanh.sem, 1)
                elif step == "tokens0":
                    act.wait_ge(bT_t.sem, bT_t.at(grp, 1))
                    later(act, kv_ps, grp, 1)
                    act.activation(bT[:, :, :, NS:BC],
                                   mixer_bank(0, grp)[:, 0:L].rearrange("p (t i n) -> p t i n", t=2,
                                                                        i=GI)[:, :, :, 0:NS],
                                   ACT.Copy).then_inc(bT_in.sem, 1)
                elif step == "states0":
                    states(0, grp)
                    states(1, grp)
                    gated(0, grp)
                elif step == "states1":
                    gated(1, grp)

            def back(e, q, grp):
                n = 2 * e + q
                act.wait_ge(hid_ps.sem, hid_ps.at(grp, n + 1))
                act.wait_ge(hw_in.sem, hw_in.at(grp, max(n - 3, 0)))
                act.activation(hid[e % 2][:, q, :], ph[q][:], ACT.Gelu, bias=b1T[:, e:e + 1]).then_inc(hid_in.sem, 1)

            def end(grp, nxt):
                if nxt is not None:
                    for q in range(2):
                        if grp is not None:
                            act.wait_ge(hid_ps.sem, hid_ps.at(grp, 2 * E))
                        act.wait_ge(fst_in[q].sem, fst_in[q].at(nxt, 1))
                        act.activation(bst[q][:], fst[q][:].bitcast(f32), ACT.Copy).then_inc(bst_in.sem, 1)
                if grp is not None:
                    act.wait_ge(done.sem, done.at(grp, E))
                    act.wait_ge(x_out.sem, x_out.at(grp, 0))
                    act.activation(ost[:], pa[:], ACT.Copy).then_inc(ost_in.sem, 1)
                    act.wait_ge(ost_in.sem, ost_in.at(grp, 1))
                    for q in range(2):
                        act.dma_start(out_v[grp, q],
                                      ost[C * q:C * q + C, :].rearrange("c (b l) -> c b l", b=2)).then_inc(x_out.sem, 16)

            run(act, front, back, end, setup)

        @block.vector
        def _(dve):
            dve.sem_inc(hw_in.sem, 1)

            def bcast(t, n):
                return t.unsqueeze(2).broadcast_to([P, t.shape[1], n])

            def setup(step):
                if step in ("tapsa", "tapsb"):
                    dve.wait_ge(d_proj, 16 * 3)
                    for t in range(4) if step == "tapsa" else range(4, TAPS):
                        dve.tensor_scalar(tapw[:, t, :], wx_raw[:], cw_x[:, t:t + 1], None, ALU.mult).then_inc(i_dve, 1)
                    if step == "tapsa":
                        return
                    dve.tensor_copy(tapw[:, TAPS, :], wz_raw[:]).then_inc(i_dve, 1)
                    dve.wait_ge(i_dve, 10)
                    for r in range(2):
                        dve.tensor_copy(taps_h[:, :, r, :], tapw[:]).then_inc(i_dve, 1)
                elif step == "low":
                    dve.wait_ge(i_dve, 12)
                    for r in range(2):
                        dve.tensor_tensor(taps_l[:, :, r, :], tapw[:], taps_h[:, :, r, :].bitcast(f32),
                                          ALU.subtract)\
                           .then_inc(i_dve, 1)
                elif step == "taps_in":
                    for n, bank in ((0, ph[0][:]), (2, pc[:]), (4, pf[:, 0, :])):
                        dve.wait_ge(i_pe, n + 1)
                        dve.tensor_copy(wT[:, n].rearrange("p s t o -> p (s t o)"),
                                        bank).then_inc(i_dve, 1)
                elif step == "norm":
                    dve.wait_ge(d_mix, 16 * MIX)
                    dve.tensor_tensor(wg[:], wo_raw[:], lng[:], ALU.mult).then_inc(i_dve, 1)
                    dve.wait_ge(i_dve, 18)
                    dve.reduce_sum(wgs[:], wg[:], axis=AX.X).then_inc(i_dve, 1)
                    dve.wait_ge(i_dve, 19)
                    dve.scalar_tensor_tensor(out=wgc[:], in0=wgs[:, 0:1].broadcast_to([C, DI]), scalar=-1.0 / DI,
                                             in1=wg[:], op0=ALU.mult, op1=ALU.add).then_inc(i_dve, 1)
                    dve.tensor_copy(lnbB[:], lnb[:, 0:1].broadcast_to([DI, P])).then_inc(i_dve, 1)
                    dve.memset(wo[:, C:OW], 1.0 / DI).then_inc(i_dve, 1)
                elif step == "experts":
                    dve.wait_ge(i_pool, POOL_ALL)
                    dve.tensor_tensor(selc[:, 0], ident[:, 0:E], ident[:, E:2 * E], ALU.add).then_inc(i_dve, 1)
                    dve.wait_ge(i_dve, 23)
                    dve.tensor_tensor(selc[:, 1], selc[:, 0], ident[:, 2 * E:3 * E], ALU.add).then_inc(i_dve, 1)
                    dve.wait_ge(i_dve, 24)
                    dve.tensor_copy(sel[:], selc[:, 1].unsqueeze(2).broadcast_to([P, E, P])).then_inc(i_dve, 1)
                    dve.wait_ge(d_exp, 16 * EXP)
                    dve.wait_ge(i_act, 9)
                    dve.tensor_tensor(w1l[:], w1_raw[:], w1h[:].bitcast(f32), ALU.subtract).then_inc(i_dve, 1)
                    R = PARTS * E
                    dve.tensor_copy(b2p[0:R, 0, :], b2_raw[:]).then_inc(i_dve, 1)
                    dve.wait_ge(i_dve, 27)
                    dve.tensor_tensor(b2f[:, 0], b2_raw[:], b2p[0:R, 0, :], ALU.subtract).then_inc(i_dve, 1)
                    dve.wait_ge(i_dve, 28)
                    dve.tensor_copy(b2p[0:R, 1, :], b2f[:, 0]).then_inc(i_dve, 1)
                    dve.wait_ge(i_dve, 29)
                    dve.tensor_tensor(b2f[:, 1], b2f[:, 0], b2p[0:R, 1, :], ALU.subtract).then_inc(i_dve, 1)
                    dve.wait_ge(i_dve, 30)
                    dve.tensor_copy(b2p[0:R, 2, :], b2f[:, 1]).then_inc(i_dve, 1)

            def centre2(grp):
                t, c, src = ln[1], ln_dve[1], x2[:]
                dve.reduce_sum(t["s1"][:], src, axis=AX.X).then_inc(c.sem, 1)
                later(dve, ln_sq[1], grp, 1)
                dve.wait_ge(c.sem, c.at(grp, 1))
                dve.scalar_tensor_tensor(out=t["xc"][:], in0=bcast(t["s1"][:], C), scalar=-1.0 / C, in1=src,
                                         op0=ALU.mult, op1=ALU.add).then_inc(c.sem, 1)

            def variance(n, grp):
                t, c = ln[n], ln_dve[n]
                dve.wait_ge(ln_sq[n].sem, ln_sq[n].at(grp, 1))
                dve.reduce_sum(t["s2"][:], t["sq"][:], axis=AX.X).then_inc(c.sem, 1)
                dve.wait_ge(c.sem, c.at(grp, CENTRE[n] + 1))
                dve.tensor_scalar(t["ve"][:], t["s2"][:], 1.0 / C, 1e-6 if n == 0 else 1e-5,
                                  ALU.mult, ALU.add).then_inc(c.sem, 1)

            def normalise(n, grp):
                t, c = ln[n], ln_dve[n]
                dve.wait_ge(ln_pow[n].sem, ln_pow[n].at(grp, 1))
                xc = t["xc"][:] if n else mixer_bank(0, grp).rearrange("p (t c) -> p t c", c=C)
                dve.tensor_tensor(t["xn"][:], xc, bcast(t["r"][:], C), ALU.mult).then_inc(c.sem, 1)

            def low(n, grp):
                t, c = ln[n], ln_dve[n]
                dve.wait_ge(ln_high[n].sem, ln_high[n].at(grp, 1))
                dve.tensor_tensor(t["hl"][:, :, 1, :], t["xn"][:], t["hl"][:, :, 0, :].bitcast(f32),
                                  ALU.subtract).then_inc(c.sem, 1)

            def convolve(row, grp):
                if row == 0:
                    dve.wait_ge(bcp_in.sem, bcp_in.at(grp, 1))
                    later(dve, bc_in, grp, 1)
                    if first(grp):
                        dve.wait_ge(d_bc, 16 * CONV)
                for t in range(3 * row, 3 * row + 3):
                    view = bcp[:, t // 3:t // 3 + HH, t % 3:t % 3 + WW]
                    if t == 0:
                        ins = dve.tensor_scalar(bcc[:], view, cw_bc[:, 0:1], None, ALU.mult)
                    else:
                        dve.wait_ge(bc_conv.sem, bc_conv.at(grp, t))
                        ins = dve.scalar_tensor_tensor(out=bcc[:], in0=view, scalar=cw_bc[:, t:t + 1], in1=bcc[:],
                                                       op0=ALU.mult, op1=ALU.add)
                    ins.then_inc(bc_conv.sem, 1)

            def softplus(part, grp):
                c = dt_dve

                def after(k):
                    dve.wait_ge(c.sem, c.at(grp, k))

                def term(k, m):
                    after(6 + k)
                    dve.scalar_tensor_tensor(out=dtp[:], in0=dtp[:], scalar=1.0 / m, in1=dtq[:],
                                             op0=ALU.add, op1=ALU.mult).then_inc(c.sem, 1)

                if part == 0:
                    dve.wait_ge(dt_exp.sem, dt_exp.at(grp, 1))
                    dve.tensor_scalar(dtd[:], dtu[:], 2.0, None, ALU.add).then_inc(c.sem, 1)
                    after(3)
                    dve.reciprocal(dtd[:], dtd[:]).then_inc(c.sem, 1)
                    after(4)
                    dve.tensor_tensor(dts[:], dtu[:], dtd[:], ALU.mult).then_inc(c.sem, 1)
                    after(5)
                    dve.tensor_tensor(dtq[:], dts[:], dts[:], ALU.mult).then_inc(c.sem, 1)
                    after(6)
                    dve.tensor_scalar(dtp[:], dtq[:], 1.0 / 13.0, None, ALU.mult).then_inc(c.sem, 1)
                    for k, m in enumerate((11, 9)):
                        term(k + 1, m)
                else:
                    for k, m in enumerate((7, 5, 3)):
                        term(k + 3, m)
                    dve.tensor_scalar(dtv[:], dtv[:], 0.0, None, ALU.max).then_inc(c.sem, 1)
                    after(12)
                    dve.scalar_tensor_tensor(out=dtp[:], in0=dtp[:], scalar=1.0, in1=dts[:],
                                             op0=ALU.add, op1=ALU.mult).then_inc(c.sem, 1)
                    after(14)
                    dve.scalar_tensor_tensor(out=dtp[:], in0=dtp[:], scalar=2.0, in1=dtv[:],
                                             op0=ALU.mult, op1=ALU.add).then_inc(c.sem, 1)
                    if first(grp):
                        dve.wait_ge(i_act, 4)
                    after(15)
                    dve.tensor_tensor(dA[:], dtp[:], expA[:].unsqueeze(1).broadcast_to([P, GI * 2, NH]),
                                      ALU.mult).then_inc(c.sem, 1)

            def route(grp):
                rankB = rank[:].unsqueeze(1).broadcast_to([P, NT, E])

                def after(k):
                    dve.wait_ge(rt.sem, rt.at(grp, k))

                dve.wait_ge(gate_ps.sem, gate_ps.at(grp, 1))
                dve.tensor_tensor(lg[:], pf[:, 1, 0:NT * E].rearrange("p (t e) -> p t e", e=E),
                                  gb[:].unsqueeze(1).broadcast_to([P, NT, E]), ALU.add).then_inc(rt.sem, 1)
                after(1)
                dve.reduce_max(m1[:], lg[:], axis=AX.X).then_inc(rt.sem, 1)
                after(2)
                dve.tensor_tensor(ld[:], lg[:], bcast(m1[:], E), ALU.subtract).then_inc(rt.sem, 1)
                after(3)
                dve.scalar_tensor_tensor(out=k1[:], in0=ld[:], scalar=0.0, in1=rankB,
                                         op0=ALU.is_ge, op1=ALU.mult).then_inc(rt.sem, 1)
                after(4)
                dve.reduce_max(kk[:], k1[:], axis=AX.X).then_inc(rt.sem, 1)
                dve.wait_ge(rt_tanh.sem, rt_tanh.at(grp, 1))
                dve.tensor_scalar(td[:], th[:], -1.0, 1.0, ALU.mult, ALU.add).then_inc(rt.sem, 1)

            def route1(grp):
                def after(k):
                    dve.wait_ge(rt.sem, rt.at(grp, k))

                after(5)
                dve.tensor_tensor(o1[:], k1[:], bcast(kk[:], E), ALU.is_equal).then_inc(rt.sem, 1)
                after(6)
                dve.reciprocal(td[:], td[:]).then_inc(rt.sem, 1)
                after(7)
                dve.scalar_tensor_tensor(out=lg2[:], in0=o1[:], scalar=-1e30, in1=ld[:],
                                         op0=ALU.mult, op1=ALU.add).then_inc(rt.sem, 1)
                after(8)
                dve.scalar_tensor_tensor(out=pe_[:], in0=th[:], scalar=1.0, in1=td[:],
                                         op0=ALU.add, op1=ALU.mult).then_inc(rt.sem, 1)
                after(9)
                dve.reduce_max(m1[:], lg2[:], axis=AX.X).then_inc(rt.sem, 1)
                after(10)
                dve.reduce_sum(ps_[:], pe_[:], axis=AX.X).then_inc(rt.sem, 1)
                after(11)
                dve.tensor_tensor(lg2[:], lg2[:], bcast(m1[:], E), ALU.subtract).then_inc(rt.sem, 1)
                after(12)
                dve.reciprocal(pr[:], ps_[:]).then_inc(rt.sem, 1)

            def route2(grp):
                rankB = rank[:].unsqueeze(1).broadcast_to([P, NT, E])

                def after(k):
                    dve.wait_ge(rt.sem, rt.at(grp, k))

                after(13)
                dve.scalar_tensor_tensor(out=k1[:], in0=lg2[:], scalar=0.0, in1=rankB,
                                         op0=ALU.is_ge, op1=ALU.mult).then_inc(rt.sem, 1)
                after(14)
                dve.tensor_tensor(pe_[:], pe_[:], bcast(pr[:], E), ALU.mult).then_inc(rt.sem, 1)
                after(15)
                dve.reduce_max(kk[:], k1[:], axis=AX.X).then_inc(rt.sem, 1)
                after(17)
                dve.tensor_tensor(o2[:], k1[:], bcast(kk[:], E), ALU.is_equal).then_inc(rt.sem, 1)
                after(18)
                dve.tensor_tensor(o1[:], o1[:], o2[:], ALU.add).then_inc(rt.sem, 1)
                after(19)
                dve.tensor_tensor(cw[:], pe_[:], o1[:], ALU.mult).then_inc(rt.sem, 1)
                after(20)
                if first(grp):
                    dve.wait_ge(i_pool, POOL_ALL)
                dve.tensor_copy(cwp[:, :, 0:E], cw[:]).then_inc(rt.sem, 1)
                after(21)
                dve.tensor_tensor(cr[:, 0], cw[:], cwp[:, :, 0:E], ALU.subtract).then_inc(rt.sem, 1)
                after(22)
                dve.tensor_copy(cwp[:, :, E:2 * E], cr[:, 0]).then_inc(rt.sem, 1)
                after(23)
                dve.tensor_tensor(cr[:, 1], cr[:, 0], cwp[:, :, E:2 * E], ALU.subtract).then_inc(rt.sem, 1)
                after(24)
                dve.tensor_copy(cwp[:, :, 2 * E:3 * E], cr[:, 1]).then_inc(rt.sem, 1)

            def tokens(q, grp):
                dve.wait_ge(dt_dve.sem, dt_dve.at(grp, 16))
                dve.wait_ge(xs_t.sem, xs_t.at(grp, q + 1))
                later(dve, kv_ps, grp, 1)
                dve.tensor_tensor(
                    v[:, q].rearrange("p j (h d) -> p (j h) d", d=HD),
                    mixer_bank(1 - q, grp).rearrange("p (n d) -> p n d", d=HD),
                    dA[:, 4 * q:4 * q + 4, :].rearrange("p a h -> p (a h)").unsqueeze(2)
                    .broadcast_to([P, TJ * NH, HD]), ALU.mult).then_inc(v_in.sem, 1)

            def states(q, grp):
                dve.wait_ge(y_ps.sem, y_ps.at(grp, q + 1))
                dve.scalar_tensor_tensor(out=gy[:, q, :], in0=xs[:, q, :], scalar=dskip[:, 0:1],
                                         in1=mixer_bank(1 - q, grp),
                                         op0=ALU.mult, op1=ALU.add).then_inc(y_dve.sem, 1)
                dve.wait_ge(y_dve.sem, y_dve.at(grp, 2 * q + 1))
                dve.wait_ge(zx_up.sem, zx_up.at(grp, q + 3))
                later(dve, o_ps, grp, 2)
                dve.tensor_tensor(g[:, q, :], gy[:, q, :], sz[:, q, :], ALU.mult).then_inc(y_dve.sem, 1)

            def front(step, grp):
                if step == "var1":
                    variance(0, grp)
                elif step == "var2":
                    variance(1, grp)
                elif step == "norm1":
                    normalise(0, grp)
                elif step == "norm2":
                    normalise(1, grp)
                elif step == "low1":
                    low(0, grp)
                elif step == "low2":
                    low(1, grp)
                elif step == "split1":
                    dve.wait_ge(split[0].sem, split[0].at(grp, 2))
                    if first(grp):
                        dve.wait_ge(i_pool, 15)
                    later(dve, zx, grp, 4)
                    dve.tensor_copy(interior(pad[1]), mixer_bank(1, grp).rearrange("p (b h w) -> p b h w", b=2, h=HH))\
                       .then_inc(padded[1].sem, 1)
                elif step == "bd":
                    dve.wait_ge(bd.sem, bd.at(grp, 1))
                    later(dve, dt_t, grp, 1)
                    dve.tensor_copy(dtc[:], mixer_bank(0, grp)[:, L:2 * L]).then_inc(dtc_in.sem, 1)
                    dve.tensor_copy(bcp[:, 1:1 + HH, 1:1 + WW],
                                    mixer_bank(0, grp)[:, 0:L].rearrange("p (h w) -> p h w", h=HH)).then_inc(bcp_in.sem, 1)
                elif step == "bdt":
                    dve.wait_ge(dt_t.sem, dt_t.at(grp, 1))
                    if first(grp):
                        dve.wait_ge(d_dt, 16 * 2)
                    dve.tensor_tensor(dtv[:].rearrange("p (i t) h -> p t i h", t=2),
                                      mixer_bank(0, grp)[:, 0:L].rearrange("p (t i n) -> p t i n", t=2,
                                                                           i=GI)[:, :, :, 0:NH],
                                      dtb[:].unsqueeze(1).unsqueeze(1).broadcast_to([P, 2, GI, NH]),
                                      ALU.add).then_inc(dt_dve.sem, 1)
                    dve.wait_ge(dt_dve.sem, dt_dve.at(grp, 1))
                    later(dve, dt_exp, grp, 1)
                    dve.scalar_tensor_tensor(out=dta[:], in0=dtv[:], scalar=-1.0, in1=dtv[:], op0=ALU.mult,
                                             op1=ALU.max).then_inc(dt_dve.sem, 1)
                elif step == "split2":
                    dve.wait_ge(split[1].sem, split[1].at(grp, 2))
                    later(dve, bst_in, grp, 2)
                    dve.tensor_copy(fst[1][:], pf[:, 1, :]).then_inc(fst_in[1].sem, 1)
                elif step in ("conv0", "conv1", "conv2"):
                    convolve(int(step[-1]), grp)
                elif step in ("soft0", "soft1"):
                    softplus(int(step[-1]), grp)
                elif step == "route":
                    route(grp)
                elif step == "route1":
                    route1(grp)
                elif step == "route2":
                    route2(grp)
                elif step in ("tokens0", "tokens1"):
                    tokens(int(step[-1]), grp)
                elif step == "states0":
                    states(0, grp)
                elif step == "states1":
                    states(1, grp)
                elif step == "weights":
                    later(dve, bcw_in, grp, 1)
                    dve.wait_ge(cw_t.sem, cw_t.at(grp, 1))
                    dve.tensor_copy(cwT[:].rearrange("p q t -> p (q t)"), pf[:, 1, :].bitcast(bf16)).then_inc(cwT_in.sem, 1)
                elif step == "output1":
                    dve.wait_ge(o_ps.sem, o_ps.at(grp, 2))
                    c = o_dve
                    mean = pf[:, 0:2, C:C + (TJ - 1) * OW + 1:OW].rearrange("p b j -> p j b")
                    square = pf[:, 0:2, TJ * OW:TJ * OW + TJ].rearrange("p b j -> p j b")
                    dve.tensor_copy(gm[:], mean).then_inc(c.sem, 1)
                    dve.wait_ge(c.sem, c.at(grp, 1))
                    dve.tensor_tensor(gmm[:], gm[:], gm[:], ALU.mult).then_inc(c.sem, 1)
                    dve.wait_ge(c.sem, c.at(grp, 2))
                    dve.tensor_tensor(gv[:], square, gmm[:], ALU.subtract).then_inc(c.sem, 1)
                    dve.wait_ge(c.sem, c.at(grp, 3))
                    dve.tensor_scalar(ge[:], gv[:], 0.0, 1e-5, ALU.max, ALU.add).then_inc(c.sem, 1)
                elif step == "residual":
                    c = o_dve
                    dve.wait_ge(o_pow.sem, o_pow.at(grp, 1))
                    for q in range(2):
                        ins = dve.tensor_tensor(
                            xo[:].rearrange("p (j q) c -> p q j c", q=2)[:, q],
                            pf[:, 1 - q, 0:TJ * OW].rearrange("p (j c) -> p j c", c=OW)[:, :, 0:C],
                            gr[:].rearrange("p (j b) -> p b j", b=2)[:, 1 - q].unsqueeze(2).broadcast_to([P, TJ, C]),
                            ALU.mult)
                    ins.then_inc(c.sem, 1)
                elif step == "sum":
                    c = o_dve
                    dve.wait_ge(c.sem, c.at(grp, 5))
                    dve.wait_ge(xpc_in.sem, xpc_in.at(grp, 1))
                    later(dve, opened, grp, 1)
                    dve.tensor_tensor(x2[:], xo[:], xpc[:], ALU.add).then_inc(c.sem, 1)
                elif step == "centre2":
                    dve.wait_ge(o_dve.sem, o_dve.at(grp, 6))
                    centre2(grp)

            def back(e, q, grp):
                n = 2 * e + q + 1
                dve.wait_ge(hid_in.sem, hid_in.at(grp, n))
                dve.wait_ge(cwb.sem, cwb.at(grp, n))
                dve.wait_ge(done.sem, done.at(grp, max(e - 1, 0)))
                dve.tensor_tensor(hw[e % 2][:, q, :], hid[e % 2][:, q, :], pc[:], ALU.mult).then_inc(hw_in.sem, 1)

            def end(grp, nxt):
                if nxt is not None:
                    if grp is not None:
                        dve.wait_ge(cwb.sem, cwb.at(grp, 2 * E))
                    dve.wait_ge(cwT_in.sem, cwT_in.at(nxt, 1))
                    dve.tensor_copy(bcw[:], cwT[:]).then_inc(bcw_in.sem, 1)

            run(dve, front, back, end, setup)

        @block.tensor
        def _(pe):
            pe.sem_inc(done.sem, 1)
            pe.wait_ge(i_pool, 8)

            def stay_busy(step, bank):
                for k in range(BUSY[step]):
                    pe.matmul(bank, wT[:, 0, 0, 0, :], wT[:, 4].rearrange("p s t o -> p (s t o)"),
                              start=True, stop=True)

            def transpose_pair(bank, k, first_, second):
                pe.matmul(bank[:, P * k:P * k + 2 * P], first_, identr[:, P:3 * P], start=True, stop=False)
                return pe.matmul(bank[:, P * k:P * k + 2 * P], second, identr[:, 0:2 * P], start=False, stop=True)

            def setup(step):
                banks = (ph[0][:], ph[1][:], pc[:], pa[:], pf[:, 0, :])
                if step in ("tapsb", "low"):
                    part = 0 if step == "tapsb" else 1
                    pe.wait_ge(i_pool, 10)
                    pe.wait_ge(i_dve, 12 + 2 * part)
                    for n in range(5):
                        ins = transpose_pair(banks[n], 2 * part,
                                             *((taps_h, taps_l)[part][:, 2 * n + k].rearrange("p r c -> p (r c)")
                                               for k in range(2)))
                        if part == 1:
                            ins.then_inc(i_pe, 1)
                    if part == 1:
                        pe.wait_ge(d_wbd, 16)
                        pe.transpose(pf[:, 1, 0:2 * BC], wbd_raw[:].rearrange("o r c -> o (r c)"),
                                     ident[0:2 * BC, 0:2 * BC]).then_inc(i_pe, 1)
                elif step in BUSY:
                    pe.wait_ge(i_dve, 17)
                    pe.wait_ge(i_act, 3 if step in ("busy0", "busy1") else ACT_ALL - 1)
                    stay_busy(step, pa[:])
                elif step == "norm_t":
                    pe.wait_ge(i_dve, 20)
                    pe.transpose(pf[:, 0, 0:C], wgc[:], ident[0:C, 0:C])
                    pe.transpose(pf[:, 0, C:2 * C], wo_raw[:], ident[0:C, 0:C])
                    pe.transpose(pf[:, 0, 2 * C:2 * C + E], b1_raw[:], ident[0:E, 0:E]).then_inc(i_pe, 1)
                elif step == "c0":
                    pe.wait_ge(i_dve, 22)
                    pe.wait_ge(i_act, ACT_ALL - 2)
                    pe.matmul(pa[:, 0:C], lnbB[:], woT[:], start=True, stop=True).then_inc(i_pe, 1)

            def tokens(q, grp):
                for j in range(TJ):
                    ins = pe.transpose(mixer_bank(1 - q, grp)[:, P * j:P * j + P], xs[:, q, P * j:P * j + P], ident[:])
                ins.then_inc(xs_t.sem, 1)

            def output_of_states(q, grp):
                for i in (2 * q, 2 * q + 1):
                    ins = pe.matmul(mixer_bank(1 - q, grp)[:, L * (i % 2):L * (i % 2) + L], kv[:, i, :], bc[:],
                                    start=True, stop=True)
                ins.then_inc(y_ps.sem, 1)

            def project_x(q, row, grp):
                for t in range(3 * row, 3 * row + 3):
                    for s in range(2):
                        ins = pe.matmul(mixer_bank(1 - q, grp), wT[:, t // 2, s, t % 2, :],
                                        pad[q][:, :, t // 3:t // 3 + HH, t % 3:t % 3 + WW],
                                        start=(t == 0 and s == 0), stop=(t == TAPS - 1 and s == 1))
                if row == 2:
                    ins.then_inc(zx.sem, 1)

            def project_z(q, grp):
                for s in range(2):
                    ins = pe.matmul(mixer_bank(1 - q, grp), wT[:, TAPS // 2, s, TAPS % 2, :], interior(pad[q]),
                                    start=(s == 0), stop=(s == 1))
                ins.then_inc(zx.sem, 1)

            def parts(n, banks, grp):
                pe.wait_ge(ln_dve[n].sem, ln_dve[n].at(grp, CENTRE[n] + 4))
                for q in range(2):
                    for j in (0, 2):
                        ins = transpose_pair(banks[q], j, *(ln[n]["hl"][:, 2 * k + q].rearrange("p r c -> p (r c)")
                                                            for k in (j, j + 1)))
                    ins.then_inc(split[n].sem, 1)

            def busy(step, grp):
                prologue = isinstance(grp, int) and grp < 2
                if step in ("norm1", "low1") and not first(grp):
                    pe.wait_ge(kept.sem, kept.at(grp, 1))
                    stay_busy(step, mixer_bank(1, grp))
                elif step in ("centre2", "var2", "norm2", "low2"):
                    pe.wait_ge(o_dve.sem, o_dve.at(grp, 5))
                    stay_busy(step, pf[:, 0, :])
                elif step == "route":
                    stay_busy(step, pf[:, 0, :])
                elif step == "z":
                    if prologue:
                        pe.wait_ge(i_act, ACT_ALL - 1)
                    stay_busy(step, pa[:] if prologue else pf[:, 0, :])

            def front(step, grp):
                busy(step, grp)
                if step == "turn":
                    pe.wait_ge(x_in.sem, x_in.at(grp, 32))
                    if not isinstance(grp, int):
                        pe.wait_ge(y_dve.sem, y_dve.at(grp - 1, 3))
                    elif grp == 1:
                        pe.wait_ge(i_dve, 17)
                        pe.wait_ge(i_act, 2)
                    for j in range(TJ):
                        ins = pe.matmul(mixer_bank(0, grp)[:, P * j:P * j + P], xin[:, P * j:P * j + P], centring[:],
                                        start=True, stop=True)
                    ins.then_inc(turned.sem, 1)
                    for j in range(TJ):
                        ins = pe.transpose(mixer_bank(1, grp)[:, P * j:P * j + P], xin[:, P * j:P * j + P], ident[:])
                    ins.then_inc(turned.sem, 1)
                elif step == "split1":
                    pe.wait_ge(kept.sem, kept.at(grp, 1))
                    parts(0, (mixer_bank(0, grp), mixer_bank(1, grp)), grp)
                elif step == "split2":
                    pe.wait_ge(o_dve.sem, o_dve.at(grp, 5))
                    parts(1, (pf[:, 0, :], pf[:, 1, :]), grp)
                elif step == "bd":
                    pe.wait_ge(padded[0].sem, padded[0].at(grp, 1))
                    pe.wait_ge(padded[1].sem, padded[1].at(grp, 1))
                    if first(grp):
                        pe.wait_ge(i_act, 3)
                        pe.wait_ge(i_dve, 17)
                    for part in range(2):
                        for i in range(GI):
                            ins = pe.matmul(mixer_bank(0, grp)[BC * i:BC * i + BC, L * part:L * part + L],
                                            wbd[:, BC * part:BC * part + BC],
                                            interior(pad[i // 2])[:, i % 2].bitcast(f32), start=True, stop=True)
                    ins.then_inc(bd.sem, 1)
                elif step == "bdt":
                    pe.wait_ge(dtc_in.sem, dtc_in.at(grp, 1))
                    pe.wait_ge(bcp_in.sem, bcp_in.at(grp, 1))
                    for t in range(2):
                        ins = pe.transpose(mixer_bank(0, grp)[:, P * t:P * t + P], dtc[:, P * t:P * t + P], ident[:])
                    ins.then_inc(dt_t.sem, 1)
                elif step in ("x0a", "x0b", "x0c"):
                    if first(grp):
                        pe.wait_ge(i_dve, 17)
                    project_x(0, "abc".index(step[-1]), grp)
                elif step in ("x1a", "x1b", "x1c"):
                    pe.wait_ge(dt_dve.sem, dt_dve.at(grp, 1))
                    project_x(1, "abc".index(step[-1]), grp)
                elif step == "z":
                    for q in range(2):
                        pe.wait_ge(zx_up.sem, zx_up.at(grp, q + 1))
                        project_z(q, grp)
                elif step == "tokens0":
                    pe.wait_ge(zx_up.sem, zx_up.at(grp, 3))
                    tokens(0, grp)
                    pe.wait_ge(zx_up.sem, zx_up.at(grp, 4))
                    pe.wait_ge(bc_in.sem, bc_in.at(grp, 1))
                    for t in range(2):
                        ins = pe.transpose(mixer_bank(0, grp)[:, P * t:P * t + P], bc[:, P * t:P * t + P], ident[:])
                    ins.then_inc(bT_t.sem, 1)
                elif step == "tokens1":
                    pe.wait_ge(bT_in.sem, bT_in.at(grp, 1))
                    tokens(1, grp)
                elif step == "states0":
                    pe.wait_ge(v_in.sem, v_in.at(grp, 2))
                    for t in range(2):
                        for i in range(GI):
                            ins = pe.matmul(mixer_bank(0, grp)[BC * i:BC * i + BC, 0:DI], bT[:, t, i, :],
                                            v[:, i // 2, 2 * (i % 2) + t, :], start=(t == 0), stop=(t == 1))
                    ins.then_inc(kv_ps.sem, 1)
                    pe.wait_ge(kv_in.sem, kv_in.at(grp, 2))
                    output_of_states(0, grp)
                elif step == "states1":
                    pe.wait_ge(kv_in.sem, kv_in.at(grp, GI))
                    output_of_states(1, grp)
                elif step in ("output0", "output1"):
                    if first(grp):
                        pe.wait_ge(i_act, ACT_ALL - 1)
                        pe.wait_ge(i_pool, POOL_ALL)
                    later(pe, cwT_in, grp, 1)
                    q = int(step[-1])
                    pe.wait_ge(y_dve.sem, y_dve.at(grp, 2 * q + 2))
                    for j in range(TJ):
                        pe.matmul(pf[:, 1 - q, OW * j:OW * j + OW], g[:, q, P * j:P * j + P], wo[:],
                                  start=True, stop=True)
                    pe.wait_ge(gsq_in.sem, gsq_in.at(grp, q + 1))
                    for j in range(TJ):
                        ins = pe.matmul(pf[:, 1 - q, TJ * OW + j:TJ * OW + j + 1], gsq[:, q, P * j:P * j + P],
                                        ones[:], start=True, stop=True)
                    ins.then_inc(o_ps.sem, 1)
                elif step == "gate":
                    pe.wait_ge(fst_in[0].sem, fst_in[0].at(grp, 1))
                    pe.wait_ge(fst_in[1].sem, fst_in[1].at(grp, 1))
                    for j in range(TJ):
                        for q in range(2):
                            n = 2 * j + q
                            ins = pe.matmul(pf[:, 1, E * n:E * n + E], fst[q][:, P * j:P * j + P].bitcast(f32), gw[:],
                                            start=True, stop=True)
                    ins.then_inc(gate_ps.sem, 1)
                elif step == "weights":
                    pe.wait_ge(rt.sem, rt.at(grp, rt.per))
                    for q in range(2):
                        for j in range(TJ):
                            ins = pe.transpose(pf[:, 1, :].bitcast(bf16)[:, HT * q + P * j:HT * q + P * j + P],
                                               cwp[:, 2 * j + q, :], identb[:])
                    ins.then_inc(cw_t.sem, 1)

            def open_output(grp):
                pe.wait_ge(ost_in.sem, ost_in.at(grp, 0))
                for s in range(PARTS):
                    for q in range(2):
                        pe.matmul(pa[C * q:C * q + C, :], b2p[:, s, :], bcw[:, q, :], start=(s == 0), stop=False)
                for j in range(TJ):
                    for q in range(2):
                        ins = pe.matmul(pa[C * q:C * q + C, P * j:P * j + P], x2[:, 2 * j + q, :], ident[:],
                                        start=False, stop=False)
                ins.then_inc(opened.sem, 1)

            def add(e, grp):
                for q in range(2):
                    pe.wait_ge(hw_in.sem, hw_in.at(grp, 2 * e + q + 1))
                for q in range(2):
                    ins = pe.matmul(pa[C * q:C * q + C, :], w2[:, e, :], hw[e % 2][:, q, :], start=False,
                                    stop=(e == E - 1))
                ins.then_inc(done.sem, 1)

            def back(e, q, grp):
                n = 2 * e + q
                if q == 0:
                    for h in range(2):
                        if e == 0:
                            pe.wait_ge(bst_in.sem, bst_in.at(grp, h + 1))
                        pe.wait_ge(hid_in.sem, hid_in.at(grp, max(n + h - 1, 0)))
                        pe.matmul(ph[h][:], w1h[:, e, :], bst[h][:], start=True, stop=False)
                        pe.matmul(ph[h][:], w1l[:, e, :], bst[h][:], start=False, stop=True).then_inc(hid_ps.sem, 1)
                elif e > 0:
                    add(e - 1, grp)
                if n == 0:
                    pe.wait_ge(bcw_in.sem, bcw_in.at(grp, 1))
                pe.wait_ge(hw_in.sem, hw_in.at(grp, n))
                pe.matmul(pc[:], sel[:, e, :], bcw[:, q, :], start=True, stop=True).then_inc(cwb.sem, 1)
                if n == 0:
                    open_output(grp)

            def end(grp, nxt):
                if grp is not None:
                    add(E - 1, grp)
                else:
                    pe.wait_ge(y_dve.sem, y_dve.at(1, 3))
                    pe.wait_ge(i_dve, 31)
                    pe.wait_ge(i_act, ACT_ALL)

            run(pe, front, back, end, setup)


_INS = ["x", "L0_conv_W_in", "L0_conv_conv_w", "L0_conv_conv_b", "L0_conv_dt_bias", "L0_conv_A_log", "L0_conv_D",
        "L0_conv_ln_g", "L0_conv_ln_b", "L0_conv_W_out", "L0_ffn_gate_w", "L0_ffn_gate_b", "L0_ffn_W1", "L0_ffn_b1",
        "L0_ffn_W2", "L0_ffn_b2"]


def kernel(**inputs):
    import numpy as _np
    import concourse.bacc as _bacc
    from concourse import mybir as _mybir
    from concourse.bass_utils import run_bass_kernel_spmd as _run

    nc = _bacc.Bacc("TRN2", target_bir_lowering=False, num_devices=1)
    arrays, args = {}, []
    for name in _INS:
        a = _np.ascontiguousarray(inputs[name])
        arrays[f"in_{name}_dram"] = a
        args.append(nc.dram_tensor(f"in_{name}_dram", a.shape, _mybir.dt.from_np(a.dtype), kind="ExternalInput").ap())
    shape = inputs["x"].shape
    out = nc.dram_tensor("out_0_dram", shape, _mybir.dt.float32, kind="ExternalOutput").ap()
    metaformer_block(nc, *args, out)
    r = _run(nc, [arrays], core_ids=[0])
    return r.results[0]["out_0_dram"]
```
